# Optimizing a Trainium2 kernel written in Bass

```python
import numpy as np
import jax
import jax.numpy as jnp

def _softmax(x, axis=-1):
    return jax.nn.softmax(x, axis=axis)

def _gelu(x):
    return jax.nn.gelu(x, approximate=True)

def _silu(x):
    return jax.nn.silu(x)

def _sigmoid(x):
    return jax.nn.sigmoid(x)

def _layernorm(x, axis=-1, eps=1e-05):
    m = jnp.mean(x, axis=axis, keepdims=True)
    v = jnp.var(x, axis=axis, keepdims=True)
    return (x - m) / jnp.sqrt(v + eps)

def _scatter_add(tgt, idx, src, axis=0):
    return tgt.at[idx].add(src)

def _segment_sum(src, seg, n):
    return jax.ops.segment_sum(src, seg, n)
kernel_name = 'mk_gnn_resnorm_d4_gnn_r8_f14692'

def setup_inputs(seed: int=0):
    np.random.seed(seed)
    _w = jnp.asarray

    def _rec_inputs():
        import jax
        import jax.numpy as jnp
        _gk = jax.random.key(seed)
        x = -0.0001006 + 1 * jax.random.normal(jax.random.fold_in(_gk, 1), (12500, 96), jnp.float32)
        _s = jax.random.randint(jax.random.fold_in(_gk, 2), (100000,), 0, 12500, jnp.int32)
        _d = jax.random.randint(jax.random.fold_in(_gk, 3), (100000,), 0, 12500, jnp.int32)
        _loop = jnp.arange(12500, dtype=jnp.int32)
        src = jnp.concatenate([_s, _d, _loop])
        dst = jnp.concatenate([_d, _s, _loop])
        _o = jnp.argsort(dst, stable=True)
        src = src[_o]
        dst = dst[_o]
        edge_attr_32 = 0.000196303 + 1.00016 * jax.random.normal(jax.random.fold_in(_gk, 12), (212500, 32), jnp.float32)
        edge_attr_96 = -4.21973e-06 + 0.0999841 * jax.random.normal(jax.random.fold_in(_gk, 13), (212500, 96), jnp.float32)
        return (x, src, dst, edge_attr_32, edge_attr_96)
    x, src, dst, edge_attr_32, edge_attr_96 = _rec_inputs()

    def _L0_gnn_setup():
        import jax, jax.numpy as jnp
        import numpy as np
        N_NODES = 6250
        N_EDGES = 100000
        IN_DIM = 96
        OUT_DIM = 96
        EDGE_DIM = 32
        BN_EPS = 1e-05
        key = jax.random.key(seed)
        ks = jax.random.split(key, 12)
        x = jax.random.normal(ks[0], (N_NODES, IN_DIM), dtype=jnp.float32)
        edge_index = jax.random.randint(ks[1], (2, N_EDGES), 0, N_NODES, dtype=jnp.int64)
        edge_attr = jax.random.normal(ks[2], (N_EDGES, EDGE_DIM), dtype=jnp.float32)
        We = jax.random.normal(ks[3], (EDGE_DIM, IN_DIM), dtype=jnp.float32) / np.sqrt(EDGE_DIM)
        be = jnp.zeros((IN_DIM,), dtype=jnp.float32)
        W1 = jax.random.normal(ks[4], (IN_DIM, OUT_DIM), dtype=jnp.float32) / np.sqrt(IN_DIM)
        b1 = jnp.zeros((OUT_DIM,), dtype=jnp.float32)
        W2 = jax.random.normal(ks[5], (OUT_DIM, OUT_DIM), dtype=jnp.float32) / np.sqrt(OUT_DIM)
        b2 = jnp.zeros((OUT_DIM,), dtype=jnp.float32)
        gamma = jnp.ones((OUT_DIM,), dtype=jnp.float32)
        beta = jnp.zeros((OUT_DIM,), dtype=jnp.float32)
        return {'x': x, 'edge_index': edge_index, 'edge_attr': edge_attr, 'We': We, 'be': be, 'W1': W1, 'b1': b1, 'W2': W2, 'b2': b2, 'gamma': gamma, 'beta': beta}
    _L0_gnn_all = _L0_gnn_setup()
    _L0_gnn_in = {k: v for k, v in _L0_gnn_all.items() if k in ('We', 'be', 'W1', 'b1', 'W2', 'b2', 'gamma', 'beta')}
    del _L0_gnn_all

    def _L1_gnn_setup():
        import jax, jax.numpy as jnp
        import numpy as np
        N_NODES = 6250
        N_EDGES = 100000
        HID = 96

        def _gelu(x):
            return jax.nn.gelu(x, approximate=False)
        key = jax.random.key(seed)
        ks = jax.random.split(key, 12)
        s = 1.0 / np.sqrt(HID)
        return {'x_feat': jax.random.normal(ks[0], (N_NODES, HID), jnp.float32), 'bases': jax.random.normal(ks[1], (N_EDGES, HID), jnp.float32) * 0.1, 'W_pre': jax.random.normal(ks[2], (HID, HID), jnp.float32) * s, 'b_pre': jax.random.normal(ks[3], (HID,), jnp.float32) * s, 'W1': jax.random.normal(ks[4], (HID, HID), jnp.float32) * s, 'b1': jax.random.normal(ks[5], (HID,), jnp.float32) * s, 'W2': jax.random.normal(ks[6], (HID, HID), jnp.float32) * s, 'b2': jax.random.normal(ks[7], (HID,), jnp.float32) * s, 'src': jax.random.randint(ks[8], (N_EDGES,), 0, N_NODES, jnp.int32), 'dst': jax.random.randint(ks[9], (N_EDGES,), 0, N_NODES, jnp.int32)}
    _L1_gnn_all = _L1_gnn_setup()
    _L1_gnn_in = {k: v for k, v in _L1_gnn_all.items() if k in ('W_pre', 'b_pre', 'W1', 'b1', 'W2', 'b2')}
    del _L1_gnn_all

    def _L2_gnn_setup():
        import jax, jax.numpy as jnp
        import numpy as np
        N, E, D = (6250, 100000, 96)
        BN_EPS = 1e-05
        key = jax.random.key(seed)
        ks = jax.random.split(key, 10)
        feature = jax.random.normal(ks[0], (N, D), dtype=jnp.float32)
        src = jax.random.randint(ks[1], (E,), 0, N, dtype=jnp.int32)
        dst = jax.random.randint(ks[2], (E,), 0, N, dtype=jnp.int32)
        W1 = jax.random.normal(ks[3], (D, D), dtype=jnp.float32) / np.sqrt(D)
        b1 = jnp.zeros((D,), dtype=jnp.float32)
        W2 = jax.random.normal(ks[4], (D, D), dtype=jnp.float32) / np.sqrt(D)
        b2 = jnp.zeros((D,), dtype=jnp.float32)
        gamma = jnp.ones((D,), dtype=jnp.float32)
        beta = jnp.zeros((D,), dtype=jnp.float32)
        eps = jnp.zeros((1,), dtype=jnp.float32)
        return {'feature': feature, 'src': src, 'dst': dst, 'W1': W1, 'b1': b1, 'W2': W2, 'b2': b2, 'gamma': gamma, 'beta': beta, 'eps': eps}
    _L2_gnn_all = _L2_gnn_setup()
    _L2_gnn_in = {k: v for k, v in _L2_gnn_all.items() if k in ('W1', 'b1', 'W2', 'b2', 'gamma', 'beta', 'eps')}
    del _L2_gnn_all

    def _L3_gnn_setup():
        import jax, jax.numpy as jnp
        import numpy as np
        N_NODES = 6250
        N_EDGES = 100000
        D = 96
        EDGE_DROP = 0.1
        key = jax.random.key(seed)
        ks = jax.random.split(key, 12)
        d2 = 2 * D
        s1 = 1.0 / np.sqrt(d2)
        s2 = 1.0 / np.sqrt(D)
        h = jax.random.normal(ks[0], (N_NODES, D), dtype=jnp.float32)
        src = jax.random.randint(ks[1], (N_EDGES,), 0, N_NODES, dtype=jnp.int32)
        dst = jax.random.randint(ks[2], (N_EDGES,), 0, N_NODES, dtype=jnp.int32)
        Wm1 = jax.random.uniform(ks[3], (d2, D), jnp.float32, -s1, s1)
        bm1 = jnp.zeros((D,), jnp.float32)
        Wm2 = jax.random.uniform(ks[4], (D, D), jnp.float32, -s2, s2)
        bm2 = jnp.zeros((D,), jnp.float32)
        Wu1 = jax.random.uniform(ks[5], (d2, D), jnp.float32, -s1, s1)
        bu1 = jnp.zeros((D,), jnp.float32)
        Wu2 = jax.random.uniform(ks[6], (D, D), jnp.float32, -s2, s2)
        bu2 = jnp.zeros((D,), jnp.float32)
        keep = 1.0 - EDGE_DROP
        drop_mask = (jax.random.uniform(ks[7], (N_EDGES, D)) < keep).astype(jnp.float32) / keep
        return {'h': h, 'Wm1': Wm1, 'bm1': bm1, 'Wm2': Wm2, 'bm2': bm2, 'Wu1': Wu1, 'bu1': bu1, 'Wu2': Wu2, 'bu2': bu2, 'drop_mask': drop_mask, 'src': src, 'dst': dst}
    _L3_gnn_all = _L3_gnn_setup()
    _L3_gnn_in = {k: v for k, v in _L3_gnn_all.items() if k in ('Wm1', 'bm1', 'Wm2', 'bm2', 'Wu1', 'bu1', 'Wu2', 'bu2')}
    del _L3_gnn_all
    return {'x': x, 'src': src, 'dst': dst, 'edge_attr_32': edge_attr_32, 'edge_attr_96': edge_attr_96, 'L0_gnn_We': _L0_gnn_in['We'], 'L0_gnn_be': _L0_gnn_in['be'], 'L0_gnn_W1': _L0_gnn_in['W1'], 'L0_gnn_b1': _L0_gnn_in['b1'], 'L0_gnn_W2': _L0_gnn_in['W2'], 'L0_gnn_b2': _L0_gnn_in['b2'], 'L0_gnn_gamma': _L0_gnn_in['gamma'], 'L0_gnn_beta': _L0_gnn_in['beta'], 'L1_gnn_W_pre': _L1_gnn_in['W_pre'], 'L1_gnn_b_pre': _L1_gnn_in['b_pre'], 'L1_gnn_W1': _L1_gnn_in['W1'], 'L1_gnn_b1': _L1_gnn_in['b1'], 'L1_gnn_W2': _L1_gnn_in['W2'], 'L1_gnn_b2': _L1_gnn_in['b2'], 'L2_gnn_W1': _L2_gnn_in['W1'], 'L2_gnn_b1': _L2_gnn_in['b1'], 'L2_gnn_W2': _L2_gnn_in['W2'], 'L2_gnn_b2': _L2_gnn_in['b2'], 'L2_gnn_gamma': _L2_gnn_in['gamma'], 'L2_gnn_beta': _L2_gnn_in['beta'], 'L2_gnn_eps': _L2_gnn_in['eps'], 'L3_gnn_Wm1': _L3_gnn_in['Wm1'], 'L3_gnn_bm1': _L3_gnn_in['bm1'], 'L3_gnn_Wm2': _L3_gnn_in['Wm2'], 'L3_gnn_bm2': _L3_gnn_in['bm2'], 'L3_gnn_Wu1': _L3_gnn_in['Wu1'], 'L3_gnn_bu1': _L3_gnn_in['bu1'], 'L3_gnn_Wu2': _L3_gnn_in['Wu2'], 'L3_gnn_bu2': _L3_gnn_in['bu2']}

def reference(x, src, dst, edge_attr_32, edge_attr_96, L0_gnn_We, L0_gnn_be, L0_gnn_W1, L0_gnn_b1, L0_gnn_W2, L0_gnn_b2, L0_gnn_gamma, L0_gnn_beta, L1_gnn_W_pre, L1_gnn_b_pre, L1_gnn_W1, L1_gnn_b1, L1_gnn_W2, L1_gnn_b2, L2_gnn_W1, L2_gnn_b1, L2_gnn_W2, L2_gnn_b2, L2_gnn_gamma, L2_gnn_beta, L2_gnn_eps, L3_gnn_Wm1, L3_gnn_bm1, L3_gnn_Wm2, L3_gnn_bm2, L3_gnn_Wu1, L3_gnn_bu1, L3_gnn_Wu2, L3_gnn_bu2):
    import jax
    import jax.numpy as jnp

    def _L0_gnn_ref(x, edge_index, edge_attr, We, be, W1, b1, W2, b2, gamma, beta):
        import jax, jax.numpy as jnp
        import numpy as np
        N_NODES = 6250
        N_EDGES = 100000
        IN_DIM = 96
        OUT_DIM = 96
        EDGE_DIM = 32
        BN_EPS = 1e-05
        src = edge_index[0]
        dst = edge_index[1]
        msg = jax.nn.relu(x[src] + edge_attr @ We + be)
        aggr = jax.ops.segment_sum(msg, dst, num_segments=x.shape[0])
        h = x + aggr
        h = jax.nn.relu(h @ W1 + b1) @ W2 + b2
        mean = jnp.mean(h, axis=0)
        var = jnp.mean(jnp.square(h - mean), axis=0)
        h = (h - mean) * jax.lax.rsqrt(var + BN_EPS) * gamma + beta
        return jax.nn.relu(h)

    def _L1_gnn_ref(x_feat, bases, W_pre, b_pre, W1, b1, W2, b2, src, dst):
        import jax, jax.numpy as jnp
        import numpy as np
        N_NODES = 6250
        N_EDGES = 100000
        HID = 96

        def _gelu(x):
            return jax.nn.gelu(x, approximate=False)
        n = x_feat.shape[0]
        h = _gelu(x_feat @ W_pre + b_pre)
        msg = h[src] * bases
        aggr = jax.ops.segment_sum(msg, dst, num_segments=n)
        x = x_feat + aggr
        y = _gelu(_gelu(x @ W1 + b1) @ W2 + b2)
        return x + y

    def _L2_gnn_ref(feature, src, dst, W1, b1, W2, b2, gamma, beta, eps):
        import jax, jax.numpy as jnp
        import numpy as np
        N, E, D = (6250, 100000, 96)
        BN_EPS = 1e-05
        n_nodes = feature.shape[0]
        pooled = jax.ops.segment_sum(feature[src], dst, num_segments=n_nodes)
        pooled = pooled + (1.0 + eps[0]) * feature
        h = jax.nn.relu(pooled @ W1 + b1) @ W2 + b2
        mean = jnp.mean(h, axis=0)
        var = jnp.var(h, axis=0)
        h = (h - mean) * jax.lax.rsqrt(var + BN_EPS) * gamma + beta
        return jax.nn.relu(h)

    def _L3_gnn_ref(h, Wm1, bm1, Wm2, bm2, Wu1, bu1, Wu2, bu2, drop_mask, src, dst):
        import jax, jax.numpy as jnp
        import numpy as np
        N_NODES = 6250
        N_EDGES = 100000
        D = 96
        EDGE_DROP = 0.1
        n = h.shape[0]
        e = jnp.concatenate([h[src], h[dst]], axis=-1)
        e = jax.nn.relu(e @ Wm1 + bm1) @ Wm2 + bm2
        e = e * drop_mask
        m = jax.ops.segment_sum(e, dst, num_segments=n)
        z = jnp.concatenate([h, m], axis=-1)
        h_new = jax.nn.relu(z @ Wu1 + bu1) @ Wu2 + bu2
        return h_new
    edge_index = jnp.stack([src, dst])
    x = _layernorm(x + _L0_gnn_ref(x, edge_index, edge_attr_32, L0_gnn_We, L0_gnn_be, L0_gnn_W1, L0_gnn_b1, L0_gnn_W2, L0_gnn_b2, L0_gnn_gamma, L0_gnn_beta), axis=-1)
    x = _layernorm(x + _L1_gnn_ref(x, edge_attr_96, L1_gnn_W_pre, L1_gnn_b_pre, L1_gnn_W1, L1_gnn_b1, L1_gnn_W2, L1_gnn_b2, src, dst), axis=-1)
    x = _layernorm(x + _L2_gnn_ref(x, src, dst, L2_gnn_W1, L2_gnn_b1, L2_gnn_W2, L2_gnn_b2, L2_gnn_gamma, L2_gnn_beta, L2_gnn_eps), axis=-1)
    x = _layernorm(x + _L3_gnn_ref(x, L3_gnn_Wm1, L3_gnn_bm1, L3_gnn_Wm2, L3_gnn_bm2, L3_gnn_Wu1, L3_gnn_bu1, L3_gnn_Wu2, L3_gnn_bu2, edge_attr_96, src, dst), axis=-1)
    return x

_drawn_inputs = setup_inputs


def setup_inputs(seed=0):
    import zlib

    import numpy as np

    out = dict(_drawn_inputs(seed))
    spreads = {'L0_gnn_be': (0.0, 0.1),
     'L0_gnn_b1': (0.0, 0.8),
     'L0_gnn_b2': (0.0, 0.8),
     'L0_gnn_gamma': (1.0, 0.2),
     'L0_gnn_beta': (0.0, 0.1),
     'L2_gnn_b1': (0.0, 0.8),
     'L2_gnn_b2': (0.0, 0.8),
     'L2_gnn_gamma': (1.0, 0.2),
     'L2_gnn_beta': (0.0, 0.1),
     'L3_gnn_bm1': (0.0, 0.8),
     'L3_gnn_bm2': (0.0, 0.8),
     'L3_gnn_bu1': (0.0, 0.1),
     'L3_gnn_bu2': (0.0, 0.1)}
    factors = {'L1_gnn_b_pre': 3.674, 'L3_gnn_Wm1': 4.273, 'L3_gnn_Wm2': 3.39}
    for name, (base, spread) in spreads.items():
        noise = np.random.default_rng([zlib.crc32(name.encode()), seed]).standard_normal(out[name].shape)
        drawn = base * np.exp(spread * noise) if base else spread * noise
        out[name] = jnp.asarray(drawn.astype(out[name].dtype))
    for name, factor in factors.items():
        out[name] = (out[name] * factor).astype(out[name].dtype)
    return out
```

```python
from contextlib import ExitStack

import concourse.bass as bass
from concourse import mybir

F32 = mybir.dt.float32
I32 = mybir.dt.int32
ALU = mybir.AluOpType
ACT = mybir.ActivationFunctionType
AX = mybir.AxisListType

P = 128
D = 96
DE = 32
J = 4
GE = P * J
WIN = 64
SLOTS = 8
ROWSLOTS = 4
UC = 5
N_CONSTS = 30
EPS = 1e-5
PRIME_ADDED = SLOTS
PRIME = 2


def chunk_uses(buffer):
    return [q for q in range(UC) if q % 2 == buffer]


def build(nc, a, n_nodes, n_groups):
    N, G = n_nodes, n_groups
    NCH = -(-N // 512)
    CB = 512
    CA = N // NCH
    NP = NCH * CB
    IT, IC = G // SLOTS, NCH // UC
    assert CA * NCH == N and IC * UC == NCH and IT * SLOTS == G and G % 4 == 0
    GP = G // 4

    with ExitStack() as ctx:
        def sb(name, shape, dt=F32):
            return ctx.enter_context(nc.sbuf_tensor(name, shape, dt))

        def sem(name):
            return ctx.enter_context(nc.semaphore(name))

        tab_h1 = nc.dram_tensor("tab_h1", (NP, D), F32, kind="Internal").ap()
        tab_x2 = nc.dram_tensor("tab_x2", (NP, D), F32, kind="Internal").ap()
        tab_a3 = nc.dram_tensor("tab_a3", (NP, D), F32, kind="Internal").ap()
        tab_b3 = nc.dram_tensor("tab_b3", (NP, D), F32, kind="Internal").ap()
        base_dram = nc.dram_tensor("base_dram", (1, G), F32, kind="Internal").ap()

        xT = sb("xT", [D, NP])
        aggT = sb("aggT", [D, NP + WIN])
        gat = sb("gat", [P, SLOTS, J * D])
        attr = sb("attr", [P, SLOTS, GE])
        idx = sb("idx", [P, SLOTS, J], I32)
        drow = sb("drow", [P, ROWSLOTS, GE], I32)
        bwin = sb("bwin", [WIN, ROWSLOTS, D])
        raw = sb("raw", [P, 2, J * D])
        msg = sb("msg", [P, 2, J * D])
        hot = sb("hot", [P, 4, J * WIN])
        hotT = sb("hotT", [WIN, 2, GE])
        hid = sb("hid", [D + 1, 2, GE])
        rel = sb("rel", [P, G * J])
        base_bc = sb("base_bc", [P, G])
        basei = sb("basei", [1, G], I32)
        buf_a = sb("buf_a", [D, 2, CB])
        buf_b = sb("buf_b", [D, 2, CB])
        nrm = sb("nrm", [P, 2, J * D])
        iota_w = sb("iota_w", [P, J * WIN])
        part = sb("part", [P, 1])
        zeros = sb("zeros", [D, CB])
        ident = sb("ident", [P, P])
        bn = sb("bn", [D, NCH * 6])
        bnv = sb("bnv", [D, 8])
        st = sb("st", [P, 2, J * 6])
        mv = sb("mv", [P, 2, J * 2])
        rstd = sb("rstd", [P, 2, J])
        vare = sb("vare", [P, 2, J])
        neg_half = sb("neg_half", [P, J])
        eps_row = sb("eps_row", [P, J])
        small = sb("small", [P, J])
        we = sb("we", [DE + 1, D])
        wpre = sb("wpre", [D + 1, D])
        wm1 = sb("wm1", [D, 2 * D])
        wm2 = sb("wm2", [D + 1, D])
        w1 = [sb(f"w1_{l}", [D, D]) for l in range(4)]
        w1m = sb("w1m", [D, D])
        w2 = [sb(f"w2_{l}", [D, D]) for l in range(4)]
        cols = sb("cols", [D, 16])
        B1, B2, GAM, BET, BM1, EPSC = [0, 1, 2, 3], [4, 5, 6, 7], {0: 8, 2: 9}, {0: 10, 2: 11}, 12, 13

        tabs = drow[:, :, :].rearrange("p s e -> p (s e)").bitcast(F32)[:, 0:2 * 2 * J * D]
        tabs = tabs.rearrange("p (b e) -> p b e", b=2)
        dst_rows_tmp = attr[0:GP, 0:4, :].bitcast(I32)
        dst_cols_tmp = gat[:, :, :].rearrange("p s e -> p (s e)").bitcast(I32)[:, 0:G * J]

        ps = [ctx.enter_context(nc.psum_tensor(f"ps{i}", [P, 512], F32)) for i in range(8)]

        consts_loaded = sem("consts_loaded")
        dst_loaded = sem("dst_loaded")
        base_stored = sem("base_stored")
        base_loaded = sem("base_loaded")
        pool_consts = sem("pool_consts")
        prep = sem("prep")
        base_min = sem("base_min")
        prep_done = sem("prep_done")
        idx_loaded = [sem(f"idx_loaded{q}") for q in range(SLOTS)]
        attr_loaded = [sem(f"attr_loaded{q}") for q in range(SLOTS)]
        row_loaded = [sem(f"row_loaded{q}") for q in range(ROWSLOTS)]
        gathered = [sem(f"gathered{q}") for q in range(SLOTS)]
        window_added = sem("window_added")
        attr_product = sem("attr_product")
        raw_ready = sem("raw_ready")
        msg_ready = sem("msg_ready")
        hot_ready = sem("hot_ready")
        hotT_ready = sem("hotT_ready")
        pre_ready = sem("pre_ready")
        hid_ready = sem("hid_ready")
        seg_done = sem("seg_done")
        h_ready = sem("h_ready")
        mm1_done = sem("mm1_done")
        t_ready = sem("t_ready")
        mm2_done = sem("mm2_done")
        u_ready = sem("u_ready")
        u_final = sem("u_final")
        bn_var_ready = sem("bn_var_ready")
        bn_rstd_ready = sem("bn_rstd_ready")
        bn_eps_added = sem("bn_eps_added")
        eps_added = sem("eps_added")
        bn_done = sem("bn_done")
        bn_chain = sem("bn_chain")
        y_ready = sem("y_ready")
        r_ready = sem("r_ready")
        tr_ready = sem("tr_ready")
        stats_ready = sem("stats_ready")
        var_ready = sem("var_ready")
        rstd_ready = sem("rstd_ready")
        n_ready = sem("n_ready")
        tx_ready = sem("tx_ready")
        xc_ready = sem("xc_ready")
        xT_written = sem("xT_written")
        agg_cleared = sem("agg_cleared")
        tail_cleared = sem("tail_cleared")
        tabmm_done = sem("tabmm_done")
        tab_ready = sem("tab_ready")
        stored = [sem("stored0"), sem("stored1")]

        n_attr = {0: 0, 1: 1, 3: 2}
        n_prod = {0: 0, 3: 1}
        n_msg = {0: 0, 1: 1, 3: 2}
        n_tab = {0: 0, 2: 1}
        per_store = [1, 1, 2, 1]

        def stored_value(l, i, q, upto):
            b = q % 2
            before = sum(per_store[k] for k in range(l)) * IC * len(chunk_uses(b))
            return 16 * (1 + before + per_store[l] * upto) + i * (16 * per_store[l] * len(chunk_uses(b)))

        def stored_all(l, b):
            return 16 * (1 + sum(per_store[k] for k in range(l + 1)) * IC * len(chunk_uses(b)))

        def chunk_free(l, i, q, sem_prime=PRIME):
            return l * NCH + sem_prime - (0 if q == 0 else 1) + q + i * UC

        def chunk_done(l, i, q, sem_prime=0):
            return l * NCH + sem_prime + q + 1 + i * UC

        def group_done(k, i, q):
            return k * G + q + 1 + i * SLOTS

        block = ctx.enter_context(nc.Block())

        @block.sync
        def _(sp):
            sp.dma_start(dst_rows_tmp, a["dst_groups"]).then_inc(dst_loaded, 16)
            sp.dma_start(dst_cols_tmp, a["dst_cols"]).then_inc(dst_loaded, 16)
            n = 0
            for dst, src in [
                (xT[:, :], a["xT"]), (we[0:DE, :], a["We"]), (we[DE:DE + 1, :], a["be"]),
                (wpre[0:D, :], a["Wpre"]), (wpre[D:D + 1, :], a["bpre"]),
                (wm1[:, 0:D], a["Wm1"][0:D, :]), (wm1[:, D:2 * D], a["Wm1"][D:2 * D, :]),
                (wm2[0:D, :], a["Wm2"]), (wm2[D:D + 1, :], a["bm2"]),
                (w1[0][:, :], a["W1_0"]), (w1[1][:, :], a["W1_1"]), (w1[2][:, :], a["W1_2"]),
                (w1[3][:, :], a["Wu1"][0:D, :]), (w1m[:, :], a["Wu1"][D:2 * D, :]),
                (w2[0][:, :], a["W2_0"]), (w2[1][:, :], a["W2_1"]), (w2[2][:, :], a["W2_2"]),
                (cols[:, 0:1], a["b1_0"]), (cols[:, 1:2], a["b1_1"]), (cols[:, 2:3], a["b1_2"]),
                (cols[:, 3:4], a["bu1"]), (cols[:, 4:5], a["b2_0"]), (cols[:, 5:6], a["b2_1"]),
                (cols[:, 6:7], a["b2_2"]), (cols[:, 7:8], a["bu2"]), (cols[:, 8:9], a["gamma_0"]),
                (cols[:, 9:10], a["gamma_2"]), (cols[:, 10:11], a["beta_0"]),
                (cols[:, 11:12], a["beta_2"]), (cols[:, 12:13], a["bm1"]),
            ]:
                sp.dma_start(dst, src).then_inc(consts_loaded, 16)
                n += 1
            sp.dma_start(w2[3][:, :], a["Wu2"]).then_inc(stored[0], 16)
            sp.dma_start(cols[:, 13:14], a["eps"].to_broadcast([D, 1])).then_inc(stored[1], 16)
            assert n == N_CONSTS
            sp.wait_ge(base_min, 1)
            sp.dma_start(base_dram.rearrange("a (p k) -> (a p) k", k=4), small[0:GP, :]).then_inc(base_stored, 16)
            sp.wait_ge(base_stored, 16)
            sp.dma_start(base_bc[:, :], base_dram.to_broadcast([P, G])).then_inc(base_loaded, 16)
            sp.wait_ge(prep_done, 1)
            for l in range(4):
                if l == 3:
                    sp.wait_ge(stored[0], stored_all(2, 0))
                    sp.wait_ge(stored[1], stored_all(2, 1))
                with sp.Fori(0, IT) as i:
                    for q in range(SLOTS):
                        sp.wait_ge(window_added, l * G + q + 1 + i * SLOTS)
                        sp.dma_start(idx[:, q, :], a["src_cols"][:, bass.ds(i * (SLOTS * J) + q * J, J)]
                                     ).then_inc(idx_loaded[q], 16)
                        if l == 0:
                            sp.dma_start(attr[0:DE, q, :], a["attr0T"][:, bass.ds(i * (SLOTS * GE) + q * GE, GE)]
                                         ).then_inc(attr_loaded[q], 16)
                        if l in (1, 3):
                            sp.dma_start(attr[:, q, 0:J * D],
                                         a["attr96"][bass.ds(i * (SLOTS * P) + q * P, P), :]
                                         ).then_inc(attr_loaded[q], 16)
                        if l == 3:
                            rs = q % ROWSLOTS
                            sp.wait_ge(window_added, l * G + q + 1 + (PRIME_ADDED - ROWSLOTS) + i * SLOTS)
                            sp.dma_start(drow[0:WIN, rs, :],
                                         a["dst_rows"][bass.ds(i * SLOTS + q, 1), :].to_broadcast([WIN, GE])
                                         ).then_inc(row_loaded[rs], 16)
                            first = sp.value_load(basei[0:1, bass.ds(i * SLOTS + q, 1)], min_val=0, max_val=N)
                            sp.dma_start(bwin[:, rs, :], tab_b3[bass.ds(first, WIN), :]
                                         ).then_inc(row_loaded[rs], 16)
                with sp.Fori(0, IC) as i:
                    for q in range(UC):
                        b = q % 2
                        rows = bass.ds(i * (UC * P) + q * P, P)
                        if l in (0, 2):
                            sp.wait_ge(tab_ready, chunk_done(n_tab[l], i, q, PRIME))
                        else:
                            sp.wait_ge(n_ready, chunk_done(l, i, q, PRIME))
                        if l == 0:
                            sp.dma_start(tab_h1.rearrange("(r j) d -> r (j d)", j=J)[rows, :],
                                         tabs[:, b, 0:J * D]).then_inc(stored[b], 16)
                        if l == 1:
                            sp.dma_start(tab_x2.rearrange("(r j) d -> r (j d)", j=J)[rows, :],
                                         nrm[:, b, :]).then_inc(stored[b], 16)
                        if l == 2:
                            sp.dma_start(tab_a3.rearrange("(r j) d -> r (j d)", j=J)[rows, :],
                                         tabs[:, b, 0:J * D]).then_inc(stored[b], 16)
                            sp.dma_start(tab_b3.rearrange("(r j) d -> r (j d)", j=J)[rows, :],
                                         tabs[:, b, J * D:2 * J * D]).then_inc(stored[b], 16)
                        if l == 3:
                            sp.dma_start(a["out"].rearrange("(r j) d -> r (j d)", j=J)[rows, :],
                                         nrm[:, b, :]).then_inc(stored[b], 16)
            for b in range(2):
                sp.wait_ge(stored[b], stored_all(3, b))

        @block.gpsimd
        def _(pool):
            pool.iota(iota_w[:, :], [[0, J], [1, WIN]], base=0, channel_multiplier=0,
                      allow_small_or_imprecise_dtypes=True).then_inc(pool_consts, 1)
            pool.iota(part[:, :], [[0, 1]], base=0, channel_multiplier=1,
                      allow_small_or_imprecise_dtypes=True).then_inc(pool_consts, 1)
            pool.memset(ident[:, :], 0.0).then_inc(pool_consts, 1)
            pool.wait_ge(pool_consts, 3)
            pool.affine_select(out=ident[:, :], in_=ident[:, :], pattern=[[-1, P]],
                               compare_op=ALU.not_equal, fill=1.0, base=0,
                               channel_multiplier=1).then_inc(pool_consts, 1)
            pool.memset(zeros[:, :], 0.0).then_inc(pool_consts, 1)
            pool.memset(neg_half[:, :], -0.5).then_inc(pool_consts, 1)
            pool.memset(eps_row[:, :], EPS).then_inc(pool_consts, 1)
            for l in range(4):
                table = [a["x"], tab_h1, tab_x2, tab_a3][l]
                if l:
                    pool.wait_ge(stored[0], stored_all(l - 1, 0))
                    pool.wait_ge(stored[1], stored_all(l - 1, 1))
                with pool.Fori(0, IT) as i:
                    for q in range(SLOTS):
                        pool.wait_ge(idx_loaded[q], 16 * (l * IT + 1) + i * 16)
                        pool.nop(nofuse=True)
                        for j in range(J):
                            pool.indirect_dma_start(
                                out=gat[:, q, j * D:(j + 1) * D], out_offset=None, in_=table,
                                in_offset=bass.IndirectOffsetOnAxis(ap=idx[:, q, j:j + 1], axis=0),
                            ).then_inc(gathered[q], 16)
                if l in (0, 2):
                    pool.wait_ge(bn_var_ready, 1 + n_tab[l])
                    pool.tensor_tensor(bnv[:, 6:7], bnv[:, 1:2], eps_row[0:D, 0:1], ALU.add).then_inc(bn_eps_added, 1)
                    pool.wait_ge(bn_eps_added, 1 + n_tab[l])
                    pool.tensor_tensor(bnv[:, 2:3], bnv[:, 6:7], neg_half[0:D, 0:1], ALU.pow
                                       ).then_inc(bn_rstd_ready, 1)
                with pool.Fori(0, IC) as i:
                    for s in range(UC + 1):
                        if s >= 1:
                            q = s - 1
                            pool.wait_ge(var_ready, chunk_done(l, i, q))
                            pool.tensor_tensor(vare[:, q % 2, :], mv[:, q % 2, 1::2], eps_row[:, :],
                                               ALU.add).then_inc(eps_added, 1)
                            pool.wait_ge(eps_added, chunk_done(l, i, q))
                            pool.tensor_tensor(rstd[:, q % 2, :], vare[:, q % 2, :], neg_half[:, :],
                                               ALU.pow).then_inc(rstd_ready, 1)
                        if l == 3:
                            continue
                        if s < UC:
                            q = s
                            pool.wait_ge(r_ready, chunk_done(l, i, q))
                            pool.tensor_copy(aggT[:, bass.ds(i * (UC * CB) + q * CB, CB)],
                                             zeros[:, :]).then_inc(agg_cleared, 1)
                        if s >= 1:
                            q = s - 1
                            pool.wait_ge(xc_ready, chunk_done(l, i, q, PRIME))
                            chunk = xT[:, bass.ds(i * (UC * CB) + q * CB, CB)]
                            pool.tensor_copy(chunk.rearrange("d (p j) -> d j p", j=J),
                                             hid[0:D, q % 2, :].rearrange("d (j p) -> d j p", j=J)
                                             ).then_inc(xT_written, 1)

        @block.tensor
        def _(pe):
            def window_sums(l, i, q, lhs):
                pe.wait_ge(hot_ready, group_done(l, i, q))
                pe.wait_ge(window_added, l * G + q - 1 + PRIME_ADDED + i * SLOTS)
                for j in range(J):
                    mm = pe.matmul(ps[q % 2][0:D, 0:WIN], lhs[:, j * D:(j + 1) * D],
                                   hot[:, q % 4, j * WIN:(j + 1) * WIN], start=(j == 0), stop=(j == J - 1))
                mm.then_inc(seg_done, 1)

            pe.wait_ge(prep_done, 1)
            pe.wait_ge(pool_consts, 7)
            for l in range(4):
                with pe.Fori(0, IT) as i:
                    for s in range(SLOTS + {0: 1, 1: 0, 2: 0, 3: 2}[l]):
                        if l == 0:
                            if s < SLOTS:
                                q = s
                                pe.wait_ge(attr_loaded[q], 16 + i * 16)
                                for j in range(J):
                                    mm = pe.matmul(ps[2 + q % 2][:, j * D:(j + 1) * D],
                                                   attr[0:DE + 1, q, j * P:(j + 1) * P], we[:, :],
                                                   start=True, stop=True)
                                mm.then_inc(attr_product, 1)
                            if s >= 1:
                                q = s - 1
                                pe.wait_ge(msg_ready, group_done(n_msg[l], i, q))
                                window_sums(l, i, q, msg[:, q % 2, :])
                        if l == 1:
                            pe.wait_ge(msg_ready, group_done(n_msg[l], i, s))
                            window_sums(l, i, s, msg[:, s % 2, :])
                        if l == 2:
                            pe.wait_ge(gathered[s], 16 * J * (l * IT + 1) + i * (16 * J))
                            window_sums(l, i, s, gat[:, s, :])
                        if l == 3:
                            if s < SLOTS:
                                q = s
                                pe.wait_ge(gathered[q], 16 * J * (l * IT + 1) + i * (16 * J))
                                pe.wait_ge(hotT_ready, group_done(0, i, q))
                                pe.matmul(ps[4 + q % 2][0:D, :], bwin[:, q % ROWSLOTS, :], hotT[:, q % 2, :],
                                          start=True, stop=False)
                                for j in range(J):
                                    mm = pe.matmul(ps[4 + q % 2][0:D, j * P:(j + 1) * P],
                                                   gat[:, q, j * D:(j + 1) * D], ident[:, :],
                                                   start=False, stop=(j == J - 1))
                                mm.then_inc(pre_ready, 1)
                            if 1 <= s <= SLOTS:
                                q = s - 1
                                pe.wait_ge(hid_ready, group_done(0, i, q))
                                for j in range(J):
                                    mm = pe.matmul(ps[2 + q % 2][:, j * D:(j + 1) * D],
                                                   hid[:, q % 2, j * P:(j + 1) * P], wm2[:, :],
                                                   start=True, stop=True)
                                mm.then_inc(attr_product, 1)
                            if s >= 2:
                                q = s - 2
                                pe.wait_ge(msg_ready, group_done(n_msg[l], i, q))
                                window_sums(l, i, q, msg[:, q % 2, :])
                pe.wait_ge(window_added, (l + 1) * G + PRIME_ADDED)
                if l:
                    pe.wait_ge(xT_written, l * NCH + PRIME)
                with pe.Fori(0, IC) as i:
                    for s in range(UC + 1):
                        if s < UC:
                            q = s
                            if l < 3:
                                pe.wait_ge(h_ready, chunk_done(l, i, q))
                                pe.matmul(ps[q % 2][0:D, 0:CA], w1[l][:, :], buf_a[:, q % 2, 0:CA],
                                          start=True, stop=True).then_inc(mm1_done, 1)
                            else:
                                chunk = bass.ds(i * (UC * CA) + q * CA, CA)
                                pe.matmul(ps[q % 2][0:D, 0:CA], w1[l][:, :], xT[:, chunk],
                                          start=True, stop=False)
                                pe.matmul(ps[q % 2][0:D, 0:CA], w1m[:, :], aggT[:, chunk],
                                          start=False, stop=True).then_inc(mm1_done, 1)
                        if s >= 1:
                            q = s - 1
                            pe.wait_ge(t_ready, chunk_done(l, i, q))
                            pe.wait_ge(u_ready, chunk_free(l, i, q))
                            pe.matmul(ps[2 + q % 2][0:D, 0:CA], w2[l][:, :], buf_b[:, q % 2, 0:CA],
                                      start=True, stop=True).then_inc(mm2_done, 1)
                with pe.Fori(0, IC) as i:
                    for s in range(UC + 2):
                        if s < UC:
                            q = s
                            pe.wait_ge(r_ready, chunk_done(l, i, q))
                            pe.wait_ge(n_ready, chunk_free(l, i, q))
                            for j in range(J):
                                mm = pe.transpose(ps[q % 2][:, j * D:(j + 1) * D], buf_b[:, q % 2, j::J],
                                                  ident[0:D, 0:D])
                            mm.then_inc(tr_ready, 1)
                        if 1 <= s <= UC and l < 3:
                            q = s - 1
                            pe.wait_ge(n_ready, chunk_done(l, i, q, PRIME))
                            pe.wait_ge(xc_ready, chunk_free(l, i, q))
                            for j in range(J):
                                mm = pe.transpose(ps[2 + q % 2][0:D, j * P:(j + 1) * P],
                                                  nrm[:, q % 2, j * D:(j + 1) * D], ident[:, :])
                            mm.then_inc(tx_ready, 1)
                        if s >= 2 and l in (0, 2):
                            q = s - 2
                            pe.wait_ge(xc_ready, chunk_done(l, i, q, PRIME))
                            pe.wait_ge(tab_ready, chunk_free(n_tab[l], i, q))
                            for j in range(J):
                                if l == 0:
                                    mm = pe.matmul(ps[4 + q % 2][:, j * D:(j + 1) * D],
                                                   hid[:, q % 2, j * P:(j + 1) * P], wpre[:, :],
                                                   start=True, stop=True)
                                else:
                                    for half in range(2):
                                        mm = pe.matmul(ps[4 + 2 * (q % 2) + half][:, j * D:(j + 1) * D],
                                                       hid[0:D, q % 2, j * P:(j + 1) * P],
                                                       wm1[:, half * D:(half + 1) * D],
                                                       start=True, stop=True)
                            mm.then_inc(tabmm_done, 1)

        @block.scalar
        def _(act):
            act.wait_ge(prep_done, 1)
            for l in range(4):
                if l == 0:
                    with act.Fori(0, IT) as i:
                        for q in range(SLOTS):
                            act.wait_ge(raw_ready, group_done(0, i, q))
                            act.activation(msg[:, q % 2, :], raw[:, q % 2, :], ACT.Relu).then_inc(msg_ready, 1)
                if l == 3:
                    act.wait_ge(xT_written, l * NCH + PRIME)
                    with act.Fori(0, IT) as i:
                        for q in range(SLOTS):
                            act.wait_ge(pre_ready, group_done(0, i, q))
                            act.activation(hid[0:D, q % 2, :], ps[4 + q % 2][0:D, :], ACT.Relu,
                                           bias=cols[:, BM1:BM1 + 1]).then_inc(hid_ready, 1)
                f1, f2 = [(ACT.Relu, ACT.Identity), (ACT.Gelu, ACT.Gelu),
                          (ACT.Relu, ACT.Identity), (ACT.Relu, ACT.Identity)][l]
                with act.Fori(0, IC) as i:
                    for s in range(UC + 1):
                        if s < UC:
                            q = s
                            act.wait_ge(mm1_done, chunk_done(l, i, q))
                            act.activation(buf_b[:, q % 2, 0:CA], ps[q % 2][0:D, 0:CA], f1,
                                           bias=cols[:, B1[l]:B1[l] + 1]).then_inc(t_ready, 1)
                        if s >= 1:
                            q = s - 1
                            act.wait_ge(mm2_done, chunk_done(l, i, q))
                            act.activation(aggT[:, bass.ds(i * (UC * CA) + q * CA, CA)],
                                           ps[2 + q % 2][0:D, 0:CA], f2,
                                           bias=cols[:, B2[l]:B2[l] + 1]).then_inc(u_ready, 1)
                if l in (0, 2):
                    act.wait_ge(bn_done, 1 + n_tab[l])
                if l == 3:
                    continue
                with act.Fori(0, IC) as i:
                    for s in range(UC + 2):
                        if s < UC and l in (0, 2):
                            q = s
                            act.activation(buf_a[:, q % 2, :], aggT[:, bass.ds(i * (UC * CB) + q * CB, CB)],
                                           ACT.Relu, bias=bnv[:, 5:6], scale=bnv[:, 4:5]).then_inc(y_ready, 1)
                        if 1 <= s <= UC:
                            q = s - 1
                            act.wait_ge(tx_ready, chunk_done(l, i, q))
                            act.wait_ge(xT_written, chunk_free(l, i, q))
                            act.activation(hid[0:D, q % 2, :], ps[2 + q % 2][0:D, :],
                                           ACT.Identity).then_inc(xc_ready, 1)
                        if s >= 2 and l in (0, 2):
                            q = s - 2
                            act.wait_ge(tabmm_done, chunk_done(n_tab[l], i, q))
                            act.wait_ge(stored[q % 2], stored_value(l, i, q, q // 2))
                            if l == 0:
                                act.activation(tabs[:, q % 2, 0:J * D], ps[4 + q % 2][:, 0:J * D],
                                               ACT.Gelu).then_inc(tab_ready, 1)
                            else:
                                act.activation(tabs[:, q % 2, 0:J * D], ps[4 + 2 * (q % 2)][:, 0:J * D],
                                               ACT.Identity)
                                act.activation(tabs[:, q % 2, J * D:2 * J * D],
                                               ps[5 + 2 * (q % 2)][:, 0:J * D],
                                               ACT.Identity).then_inc(tab_ready, 1)

        @block.vector
        def _(dve):
            chain = [0]

            def link(ins, s=prep):
                chain[0] += 1
                ins.then_inc(prep, 1)
                dve.wait_ge(prep, chain[0])

            dve.wait_ge(dst_loaded, 32)
            dve.tensor_reduce(small[0:GP, :], dst_rows_tmp, AX.X, ALU.min).then_inc(base_min, 1)
            dve.wait_ge(base_min, 1)
            link(dve.memset(attr[DE:DE + 1, :, :], 1.0))
            link(dve.memset(hid[D:D + 1, :, :], 1.0))
            link(dve.memset(aggT[:, :], 0.0))
            dve.wait_ge(base_loaded, 16)
            dve.wait_ge(pool_consts, 7)
            link(dve.tensor_tensor(rel[:, :].rearrange("p (g j) -> p g j", j=J),
                                   dst_cols_tmp.rearrange("p (g j) -> p g j", j=J),
                                   base_bc[:, :].unsqueeze(2).to_broadcast([P, G, J]), ALU.subtract))
            link(dve.tensor_copy(basei[:, :], base_bc[0:1, :]))
            link(dve.tensor_scalar(base_bc[:, :], base_bc[:, :], part[:, 0:1], None, ALU.add))
            dve.wait_ge(consts_loaded, 16 * N_CONSTS)
            dve.wait_ge(stored[0], 16)
            dve.wait_ge(stored[1], 16)
            link(dve.tensor_scalar(cols[:, 14:15], cols[:, EPSC:EPSC + 1], 1.0, None, ALU.add))
            for primed, by in [(window_added, PRIME_ADDED), (u_ready, PRIME), (n_ready, PRIME),
                               (xc_ready, PRIME), (xT_written, PRIME), (tab_ready, PRIME)]:
                dve.sem_inc(primed, by)
            dve.sem_inc(prep_done, 1)

            def build_hot(l, i, q):
                out = hot[:, q % 4, :].rearrange("p (j w) -> p j w", j=J)
                dve.tensor_tensor(out, iota_w[:, :].rearrange("p (j w) -> p j w", j=J),
                                  rel[:, bass.ds(i * (SLOTS * J) + q * J, J)].unsqueeze(2)
                                  .to_broadcast([P, J, WIN]), ALU.is_equal).then_inc(hot_ready, 1)

            def add_window(l, i, q):
                first = dve.value_load(basei[0:1, bass.ds(i * SLOTS + q, 1)], min_val=0, max_val=N)
                dve.wait_ge(seg_done, group_done(l, i, q))
                dve.wait_ge(window_added, l * G + q + PRIME_ADDED + i * SLOTS)
                window = aggT[:, bass.ds(first, WIN)]
                dve.tensor_tensor(window, window, ps[q % 2][0:D, 0:WIN], ALU.add).then_inc(window_added, 1)

            for l in range(4):
                with dve.Fori(0, IT) as i:
                    for s in range(SLOTS + (2 if l == 3 else 1)):
                        if s < SLOTS:
                            q = s
                            build_hot(l, i, q)
                            if l == 0:
                                dve.wait_ge(gathered[q], 16 * J + i * (16 * J))
                                dve.wait_ge(attr_product, group_done(0, i, q))
                                dve.tensor_tensor(raw[:, q % 2, :], ps[2 + q % 2][:, 0:J * D], gat[:, q, :],
                                                  ALU.add).then_inc(raw_ready, 1)
                            if l == 1:
                                dve.wait_ge(gathered[q], 16 * J * (l * IT + 1) + i * (16 * J))
                                dve.wait_ge(attr_loaded[q], 16 * (n_attr[l] * IT + 1) + i * 16)
                                dve.tensor_tensor(msg[:, q % 2, :], gat[:, q, :], attr[:, q, 0:J * D],
                                                  ALU.mult).then_inc(msg_ready, 1)
                            if l == 3:
                                rs = q % ROWSLOTS
                                dve.wait_ge(row_loaded[rs], 32 * (q // ROWSLOTS + 1) + i * (32 * SLOTS // ROWSLOTS))
                                dve.tensor_scalar(hotT[:, q % 2, :], drow[0:WIN, rs, :],
                                                  base_bc[0:WIN, bass.ds(i * SLOTS + q, 1)], None,
                                                  ALU.is_equal).then_inc(hotT_ready, 1)
                        if l == 3 and 1 <= s <= SLOTS:
                            q = s - 1
                            dve.wait_ge(attr_loaded[q], 16 * (n_attr[l] * IT + 1) + i * 16)
                            dve.wait_ge(attr_product, group_done(1, i, q))
                            dve.tensor_tensor(msg[:, q % 2, :], ps[2 + q % 2][:, 0:J * D],
                                              attr[:, q, 0:J * D], ALU.mult).then_inc(msg_ready, 1)
                        lag = 2 if l == 3 else 1
                        if s >= lag:
                            add_window(l, i, s - lag)
                dve.wait_ge(window_added, (l + 1) * G + PRIME_ADDED)
                if l:
                    dve.wait_ge(xT_written, l * NCH + PRIME)
                if l < 3:
                    with dve.Fori(0, IC) as i:
                        for s in range(UC + 1):
                            if s < UC:
                                q = s
                                chunk = bass.ds(i * (UC * CA) + q * CA, CA)
                                h = buf_a[:, q % 2, 0:CA]
                                if l == 1:
                                    dve.wait_ge(u_final, chunk_free(l, i, q, 0))
                                if l == 2:
                                    dve.scalar_tensor_tensor(out=h, in0=xT[:, chunk], scalar=cols[:, 14:15],
                                                             in1=aggT[:, chunk], op0=ALU.mult,
                                                             op1=ALU.add).then_inc(h_ready, 1)
                                else:
                                    dve.tensor_tensor(h, xT[:, chunk], aggT[:, chunk],
                                                      ALU.add).then_inc(h_ready, 1)
                            if s >= 1:
                                q = s - 1
                                chunk = bass.ds(i * (UC * CA) + q * CA, CA)
                                dve.wait_ge(u_ready, chunk_done(l, i, q, PRIME))
                                if l == 1:
                                    dve.tensor_tensor(aggT[:, chunk], aggT[:, chunk], buf_a[:, q % 2, 0:CA],
                                                      ALU.add).then_inc(u_final, 1)
                                else:
                                    dve.bn_stats(bn[:, bass.ds(i * (UC * 6) + q * 6, 6)],
                                                 aggT[:, chunk]).then_inc(u_final, 1)
                    dve.wait_ge(u_final, (l + 1) * NCH)
                else:
                    dve.wait_ge(u_ready, (l + 1) * NCH + PRIME)
                if l in (0, 2):
                    link(dve.bn_aggr(bnv[:, 0:2], bn[:, :]))
                    dve.sem_inc(bn_var_ready, 1)
                    dve.wait_ge(bn_rstd_ready, 1 + n_tab[l])
                    link(dve.tensor_tensor(bnv[:, 4:5], bnv[:, 2:3], cols[:, GAM[l]:GAM[l] + 1], ALU.mult))
                    link(dve.tensor_tensor(bnv[:, 3:4], bnv[:, 0:1], bnv[:, 4:5], ALU.mult))
                    dve.tensor_tensor(bnv[:, 5:6], cols[:, BET[l]:BET[l] + 1], bnv[:, 3:4],
                                      ALU.subtract).then_inc(bn_done, 1)
                with dve.Fori(0, IC) as i:
                    for s in range(UC + 1):
                        if s < UC:
                            q = s
                            chunk = bass.ds(i * (UC * CB) + q * CB, CB)
                            if l in (0, 2):
                                dve.wait_ge(y_ready, chunk_done(n_tab[l], i, q))
                                y = buf_a[:, q % 2, :]
                            else:
                                y = aggT[:, chunk]
                            dve.tensor_tensor(buf_b[:, q % 2, :], y, xT[:, chunk],
                                              ALU.add).then_inc(r_ready, 1)
                        if s >= 1:
                            q = s - 1
                            b = q % 2
                            dve.wait_ge(tr_ready, chunk_done(l, i, q))
                            for j in range(J):
                                ins = dve.bn_stats(st[:, b, 6 * j:6 * j + 6], ps[b][:, j * D:(j + 1) * D])
                            ins.then_inc(stats_ready, 1)
                            dve.wait_ge(stats_ready, chunk_done(l, i, q))
                            dve.nop(nofuse=True)
                            for j in range(J):
                                ins = dve.bn_aggr(mv[:, b, 2 * j:2 * j + 2], st[:, b, 6 * j:6 * j + 6])
                            ins.then_inc(var_ready, 1)
                            dve.wait_ge(rstd_ready, chunk_done(l, i, q))
                            if l in (1, 3):
                                dve.wait_ge(stored[b], stored_value(l, i, q, q // 2))
                            for j in range(J):
                                ins = dve.tensor_scalar(nrm[:, b, j * D:(j + 1) * D], ps[b][:, j * D:(j + 1) * D],
                                                        mv[:, b, 2 * j:2 * j + 1], rstd[:, b, j:j + 1],
                                                        ALU.subtract, ALU.mult)
                            ins.then_inc(n_ready, 1)
                if l < 3:
                    dve.wait_ge(agg_cleared, (l + 1) * NCH)
                    link(dve.memset(aggT[:, NP:NP + WIN], 0.0))


_SHAPES = {
    "We": (DE, D), "be": (1, D), "Wpre": (D, D), "bpre": (1, D), "Wm1": (2 * D, D), "Wm2": (D, D),
    "bm2": (1, D), "Wu1": (2 * D, D), "Wu2": (D, D), "bu1": (D, 1), "bu2": (D, 1), "bm1": (D, 1),
    "eps": (1, 1),
    "W1_0": (D, D), "W2_0": (D, D), "W1_1": (D, D), "W2_1": (D, D), "W1_2": (D, D), "W2_2": (D, D),
    "b1_0": (D, 1), "b2_0": (D, 1), "b1_1": (D, 1), "b2_1": (D, 1), "b1_2": (D, 1), "b2_2": (D, 1),
    "gamma_0": (D, 1), "beta_0": (D, 1), "gamma_2": (D, 1), "beta_2": (D, 1),
}
_NAMES = {
    "We": "L0_gnn_We", "be": "L0_gnn_be", "Wpre": "L1_gnn_W_pre", "bpre": "L1_gnn_b_pre",
    "Wm1": "L3_gnn_Wm1", "Wm2": "L3_gnn_Wm2", "bm2": "L3_gnn_bm2", "Wu1": "L3_gnn_Wu1",
    "Wu2": "L3_gnn_Wu2", "bu1": "L3_gnn_bu1", "bu2": "L3_gnn_bu2", "bm1": "L3_gnn_bm1",
    "eps": "L2_gnn_eps",
    **{f"{w}{k}_{l}": f"L{l}_gnn_{w}{k}" for l in range(3) for w in "Wb" for k in "12"},
    **{f"{w}_{l}": f"L{l}_gnn_{w}" for l in (0, 2) for w in ("gamma", "beta")},
}


def layout(inputs):
    import numpy as np

    x = np.asarray(inputs["x"])
    src, dst = np.asarray(inputs["src"]), np.asarray(inputs["dst"])
    n, e = x.shape[0], src.shape[0]
    nch = -(-n // 512)
    n_pad = nch * 512
    groups = -(-e // (GE * SLOTS)) * SLOTS
    e_pad = groups * GE

    def padded(v, rows, fill=0):
        out = np.full((rows,) + v.shape[1:], fill, v.dtype)
        out[:v.shape[0]] = v
        return out

    xp = padded(x, n_pad)
    srcp, dstp = padded(src, e_pad), padded(dst, e_pad, n)
    ea32, ea96 = padded(np.asarray(inputs["edge_attr_32"]), e_pad), padded(np.asarray(inputs["edge_attr_96"]), e_pad)
    arrays = {
        "x": xp,
        "xT": np.ascontiguousarray(xp.T),
        "src_cols": np.ascontiguousarray(srcp.reshape(groups, P, J).transpose(1, 0, 2)).reshape(P, groups * J),
        "dst_cols": np.ascontiguousarray(dstp.reshape(groups, P, J).transpose(1, 0, 2)).reshape(P, groups * J),
        "dst_groups": dstp.reshape(groups // 4, 4, GE),
        "dst_rows": np.ascontiguousarray(dstp.reshape(groups, P, J).transpose(0, 2, 1)).reshape(groups, GE),
        "attr0T": np.ascontiguousarray(ea32.reshape(groups, P, J, DE).transpose(3, 0, 2, 1)).reshape(DE, e_pad),
        "attr96": ea96.reshape(groups * P, J * D),
    }
    for name, of in _NAMES.items():
        arrays[name] = np.ascontiguousarray(np.asarray(inputs[of]).reshape(_SHAPES[name]))
    return arrays, n, groups, n_pad


def kernel(**inputs):
    import concourse.bacc as bacc
    from concourse.bass_utils import run_bass_kernel_spmd

    arrays, n, groups, n_pad = layout(inputs)
    nc = bacc.Bacc("TRN2", target_bir_lowering=False, num_devices=1)
    aps = {k: nc.dram_tensor(f"in_{k}", v.shape, mybir.dt.from_np(v.dtype), kind="ExternalInput").ap()
           for k, v in arrays.items()}
    aps["out"] = nc.dram_tensor("out_x", (n_pad, D), F32, kind="ExternalOutput").ap()
    build(nc, aps, n, groups)
    result = run_bass_kernel_spmd(nc, [{f"in_{k}": v for k, v in arrays.items()}], core_ids=[0])
    return result.results[0]["out_x"][:n]
```

```python
from contextlib import ExitStack

import concourse.bass as bass
from concourse import mybir

F32 = mybir.dt.float32
I32 = mybir.dt.int32
ALU = mybir.AluOpType
ACT = mybir.ActivationFunctionType
AX = mybir.AxisListType

P = 128
D = 96
DE = 32
J = 4
GE = P * J
CB = P * J
WIN = 64
SLOTS = 8
ROWSLOTS = 4
EPS = 1e-5
PRIME = 2

_BLOCKS = [("Wpre", D), ("Wm2", D), ("We", D), ("Wm1a", D), ("Wm1b", D), ("W1_0", D), ("W1_1", D),
           ("W1_2", D), ("Wu1a", D), ("Wu1b", D), ("W2_0", D), ("W2_1", D), ("W2_2", D), ("Wu2", D),
           ("b1_0", 1), ("b1_1", 1), ("b1_2", 1), ("bu1", 1), ("b2_0", 1), ("b2_1", 1), ("b2_2", 1),
           ("bu2", 1), ("gamma_0", 1), ("beta_0", 1), ("gamma_2", 1), ("beta_2", 1), ("bm1", 1),
           ("eps", 1)]
COL = {name: (sum(wd for _, wd in _BLOCKS[:k]), width) for k, (name, width) in enumerate(_BLOCKS)}
WCOLS = sum(width for _, width in _BLOCKS)


class Step:

    def __init__(self, const, i=None, stride=0):
        self.const, self.i, self.stride = const, i, stride

    def back(self, n):
        return Step(self.const - n, self.i, self.stride)

    def within(self, total):
        return self.i is not None or 0 <= self.const < total

    def value(self, scale=1, plus=0):
        if self.i is None:
            return self.const * scale + plus
        return self.i * (self.stride * scale) + (self.const * scale + plus)

    def slot(self, n):
        return self.const % n

    def uses(self, n):
        return Step(self.const // n, self.i, self.stride // n)


def steps(eng, total, lag, unroll):
    for s in range(lag):
        yield Step(s)
    loops = (total - lag) // unroll
    with eng.Fori(0, loops) as i:
        for s in range(unroll):
            yield Step(lag + s, i, unroll)
    for s in range(lag + loops * unroll, total + lag):
        yield Step(s)


def build(nc, a, n_nodes, n_groups):
    N, G = n_nodes, n_groups
    NCH = -(-N // CB)
    CA = N // NCH
    NP = NCH * CB
    assert CA * NCH == N and G % SLOTS == 0
    GP = G // SLOTS

    with ExitStack() as ctx:
        def sb(name, shape, dt=F32):
            return ctx.enter_context(nc.sbuf_tensor(name, shape, dt))

        def sem(name):
            return ctx.enter_context(nc.semaphore(name))

        tab_h1 = nc.dram_tensor("tab_h1", (NP, D), F32, kind="Internal").ap()
        tab_x2 = nc.dram_tensor("tab_x2", (NP, D), F32, kind="Internal").ap()
        tab_a3 = nc.dram_tensor("tab_a3", (NP, D), F32, kind="Internal").ap()
        tab_b3 = nc.dram_tensor("tab_b3", (NP, D), F32, kind="Internal").ap()
        bounds_dram = nc.dram_tensor("bounds_dram", (2, G), F32, kind="Internal").ap()

        xT = sb("xT", [D, NP])
        aggT = sb("aggT", [D, NP + WIN])
        gat = sb("gat", [P, SLOTS, J * D])
        attr = sb("attr", [P, SLOTS, GE])
        idx = sb("idx", [P, SLOTS, J], I32)
        drow = sb("drow", [P, ROWSLOTS, GE], I32)
        bwin = sb("bwin", [WIN, ROWSLOTS, D])
        raw = sb("raw", [P, 2, J * D])
        msg = sb("msg", [P, 2, J * D])
        hot = sb("hot", [P, 4, J * WIN])
        hotT = sb("hotT", [WIN, 2, GE])
        hid = sb("hid", [D + 1, 2, GE])
        rel = sb("rel", [P, G * J])
        first_bc = sb("first_bc", [P, G])
        first_i = sb("first_i", [1, G + 1], I32)
        buf_a = sb("buf_a", [D, 2, CB])
        buf_b = sb("buf_b", [D, 2, CB])
        nrm = sb("nrm", [P, 2, J * D])
        iota = sb("iota", [P, CB])
        part = sb("part", [P, 1])
        chunk0 = sb("chunk0", [P, NCH])
        ident = sb("ident", [P, P])
        bn = sb("bn", [D, NCH * 6])
        bnv = sb("bnv", [D, 8])
        st = sb("st", [P, 2, J * 6])
        mv = sb("mv", [P, 2, J * 2])
        vare = sb("vare", [P, 2, J])
        rstd = sb("rstd", [P, 2, J])
        neg_half = sb("neg_half", [P, J])
        eps_row = sb("eps_row", [P, J])
        lo = sb("lo", [P, SLOTS])
        hi = sb("hi", [P, SLOTS])
        span = sb("span", [P, SLOTS])
        off = sb("off", [P, J])
        w = sb("w", [P, WCOLS])

        def wt(name, rows=D):
            at, width = COL[name]
            return w[0:rows, at:at + width]

        xT_words = xT[:, :].bitcast(I32)
        dst_rows_tmp = xT_words[0:GP, 0:SLOTS * GE].rearrange("p (k e) -> p k e", k=SLOTS)
        tabs = drow[:, :, :].rearrange("p s e -> p (s e)").bitcast(F32)[:, 0:4 * J * D]
        tabs = tabs.rearrange("p (b e) -> p b e", b=2)
        dst_cols_tmp = drow[:, :, :].rearrange("p s e -> p (s e)")[:, 0:G * J]
        hot_wide = drow[:, :, :].rearrange("p s e -> p (s e)").bitcast(F32)
        spans = buf_a[0:1, :, :].rearrange("a b e -> a (b e)")[:, 0:G]

        ps = [ctx.enter_context(nc.psum_tensor(f"ps{i}", [P, 512], F32)) for i in range(8)]

        weights_loaded = sem("weights_loaded")
        dst_loaded = sem("dst_loaded")
        x_loaded = sem("x_loaded")
        bounds_found = sem("bounds_found")
        bounds_stored = sem("bounds_stored")
        bounds_loaded = sem("bounds_loaded")
        pool_consts = sem("pool_consts")
        prep = sem("prep")
        prep_done = sem("prep_done")
        idx_loaded = [sem(f"idx_loaded{q}") for q in range(SLOTS)]
        attr_loaded = [sem(f"attr_loaded{q}") for q in range(SLOTS)]
        gathered = [sem(f"gathered{q}") for q in range(SLOTS)]
        row_loaded = [sem(f"row_loaded{q}") for q in range(ROWSLOTS)]
        attr_product = sem("attr_product")
        raw_ready = sem("raw_ready")
        msg_ready = sem("msg_ready")
        hot_ready = sem("hot_ready")
        hotT_ready = sem("hotT_ready")
        pre_ready = sem("pre_ready")
        hid_ready = sem("hid_ready")
        seg_done = sem("seg_done")
        window_added = sem("window_added")
        mm1_done = sem("mm1_done")
        t_ready = sem("t_ready")
        mm2_done = sem("mm2_done")
        u_ready = sem("u_ready")
        u_final = sem("u_final")
        bn_var_ready = sem("bn_var_ready")
        bn_eps_added = sem("bn_eps_added")
        bn_rstd_ready = sem("bn_rstd_ready")
        bn_done = sem("bn_done")
        y_ready = sem("y_ready")
        r_ready = sem("r_ready")
        tr_ready = sem("tr_ready")
        stats_ready = sem("stats_ready")
        var_ready = sem("var_ready")
        eps_added = sem("eps_added")
        rstd_ready = sem("rstd_ready")
        n_ready = sem("n_ready")
        tx_ready = sem("tx_ready")
        xc_ready = sem("xc_ready")
        tabmm_done = sem("tabmm_done")
        tab_ready = sem("tab_ready")
        stored = [sem("stored0"), sem("stored1")]
        slow_loaded = sem("slow_loaded")
        slow_gathered = sem("slow_gathered")
        slow_prod = sem("slow_prod")
        slow_pre = sem("slow_pre")
        slow_hid = sem("slow_hid")
        slow_raw = sem("slow_raw")
        slow_msg = sem("slow_msg")
        slow_off = sem("slow_off")
        slow_hot = sem("slow_hot")
        slow_seg = sem("slow_seg")
        slow_added = sem("slow_added")
        slow_done = sem("slow_done")

        n_attr = {0: 0, 1: 1, 3: 2}
        n_prod = {0: 0, 3: 1}
        n_tab = {0: 0, 2: 1}
        per_store = [1, 1, 2, 1]
        slow_loads = [3, 3, 2, 3]
        slow_gathers = [J, J, J, 2 * J]

        def chunks_of(b):
            return -(-(NCH - b) // 2)

        def stored_before(l, c):
            b = c.slot(2)
            base = 16 * (1 + sum(per_store[:l]) * chunks_of(b))
            return c.uses(2).value(16 * per_store[l], base)

        def stored_all(l, b):
            return 16 * (1 + sum(per_store[:l + 1]) * chunks_of(b))

        def slot_value(g, layers, per):
            return g.uses(SLOTS).value(per, per * (layers * (G // SLOTS) + 1))

        def is_general(eng):
            return eng.value_load(first_i[0:1, G:G + 1], min_val=0, max_val=1)

        block = ctx.enter_context(nc.Block())

        @block.sync
        def _(sp):
            sp.dma_start(dst_rows_tmp, a["dst_groups"]).then_inc(dst_loaded, 16)
            sp.dma_start(dst_cols_tmp, a["dst_cols"]).then_inc(dst_loaded, 16)
            half = WCOLS // 2
            sp.dma_start(w[:, 0:half], a["weights"][:, 0:half]).then_inc(stored[0], 16)
            sp.dma_start(w[:, half:WCOLS], a["weights"][:, half:WCOLS]).then_inc(stored[1], 16)
            sp.wait_ge(bounds_found, 2)
            sp.dma_start(bounds_dram[0:1, :].rearrange("a (p k) -> (a p) k", k=SLOTS), lo[0:GP, :]
                         ).then_inc(bounds_stored, 16)
            sp.dma_start(bounds_dram[1:2, :].rearrange("a (p k) -> (a p) k", k=SLOTS), span[0:GP, :]
                         ).then_inc(bounds_stored, 16)
            sp.dma_start(aggT[:, 0:NP], a["xT"]).then_inc(x_loaded, 16)
            sp.wait_ge(bounds_stored, 32)
            sp.dma_start(first_bc[:, :], bounds_dram[0:1, :].to_broadcast([P, G])).then_inc(bounds_loaded, 16)
            sp.dma_start(spans, bounds_dram[1:2, :]).then_inc(bounds_loaded, 16)
            sp.dma_start(xT[:, :], a["xT"]).then_inc(x_loaded, 16)
            sp.wait_ge(prep_done, 1)
            general = is_general(sp)

            def load_group(l, g):
                q = g.slot(SLOTS)
                sp.wait_ge(window_added, g.value(1, l * G + 1))
                sp.dma_start(idx[:, q, :], a["src_cols"][:, bass.ds(g.value(J), J)]).then_inc(idx_loaded[q], 16)
                if l == 0:
                    sp.dma_start(attr[0:DE, q, :], a["attr0T"][:, bass.ds(g.value(GE), GE)]
                                 ).then_inc(attr_loaded[q], 16)
                if l in (1, 3):
                    sp.dma_start(attr[:, q, 0:J * D], a["attr96"][bass.ds(g.value(P), P), :]
                                 ).then_inc(attr_loaded[q], 16)
                if l == 3:
                    rs = g.slot(ROWSLOTS)
                    sp.wait_ge(pre_ready, g.value(1, 1))
                    sp.dma_start(drow[0:WIN, rs, :], a["dst_rows"][bass.ds(g.value(), 1), :].to_broadcast([WIN, GE])
                                 ).then_inc(row_loaded[rs], 16)
                    first = sp.value_load(first_i[0:1, bass.ds(g.value(), 1)], min_val=0, max_val=N)
                    sp.dma_start(bwin[:, rs, :], tab_b3[bass.ds(first, WIN), :]).then_inc(row_loaded[rs], 16)

            for l in range(4):
                if l == 3:
                    sp.wait_ge(stored[0], stored_all(2, 0))
                    sp.wait_ge(stored[1], stored_all(2, 1))
                with sp.If(general == 0):
                    for g in steps(sp, G, 0, SLOTS):
                        load_group(l, g)
                with sp.Else():
                    with sp.Fori(0, G) as i:
                        g = Step(0, i, 1)
                        sp.wait_ge(slow_done, g.value(1, l * G + 1))
                        sp.dma_start(idx[:, 0, :], a["src_cols"][:, bass.ds(g.value(J), J)]).then_inc(slow_loaded, 16)
                        sp.dma_start(idx[:, 1, :], a["dst_cols"][:, bass.ds(g.value(J), J)]).then_inc(slow_loaded, 16)
                        if l == 0:
                            sp.dma_start(attr[0:DE, 0, :], a["attr0T"][:, bass.ds(g.value(GE), GE)]
                                         ).then_inc(slow_loaded, 16)
                        if l in (1, 3):
                            sp.dma_start(attr[:, 0, 0:J * D], a["attr96"][bass.ds(g.value(P), P), :]
                                         ).then_inc(slow_loaded, 16)
                for c in steps(sp, NCH, 0, 2):
                    b = c.slot(2)
                    rows = bass.ds(c.value(P), P)
                    if l in (0, 2):
                        sp.wait_ge(tab_ready, c.value(1, n_tab[l] * NCH + PRIME + 1))
                    else:
                        sp.wait_ge(n_ready, c.value(1, l * NCH + PRIME + 1))
                    for table, source in {
                        0: [(tab_h1, tabs[:, b, 0:J * D])],
                        1: [(tab_x2, nrm[:, b, :])],
                        2: [(tab_a3, tabs[:, b, 0:J * D]), (tab_b3, tabs[:, b, J * D:2 * J * D])],
                        3: [(a["out"], nrm[:, b, :])],
                    }[l]:
                        sp.dma_start(table.rearrange("(r j) d -> r (j d)", j=J)[rows, :], source
                                     ).then_inc(stored[b], 16)
            for b in range(2):
                sp.wait_ge(stored[b], stored_all(3, b))

        @block.gpsimd
        def _(pool):
            pool.iota(iota[:, :], [[1, CB]], base=0, channel_multiplier=0,
                      allow_small_or_imprecise_dtypes=True).then_inc(pool_consts, 1)
            pool.iota(chunk0[:, :], [[CB, NCH]], base=0, channel_multiplier=0,
                      allow_small_or_imprecise_dtypes=True).then_inc(pool_consts, 1)
            pool.iota(part[:, :], [[0, 1]], base=0, channel_multiplier=1,
                      allow_small_or_imprecise_dtypes=True).then_inc(pool_consts, 1)
            pool.memset(neg_half[:, :], -0.5).then_inc(pool_consts, 1)
            pool.memset(eps_row[:, :], EPS).then_inc(pool_consts, 1)
            pool.memset(ident[:, :], 0.0).then_inc(pool_consts, 1)
            pool.wait_ge(pool_consts, 6)
            pool.affine_select(out=ident[:, :], in_=ident[:, :], pattern=[[-1, P]],
                               compare_op=ALU.not_equal, fill=1.0, base=0,
                               channel_multiplier=1).then_inc(pool_consts, 1)
            pool.wait_ge(prep_done, 1)
            general = is_general(pool)

            def gather(table, to, indices, done):
                for j in range(J):
                    pool.indirect_dma_start(
                        out=gat[:, to, j * D:(j + 1) * D], out_offset=None, in_=table,
                        in_offset=bass.IndirectOffsetOnAxis(ap=idx[:, indices, j:j + 1], axis=0),
                    ).then_inc(done, 16)

            for l in range(4):
                table = [a["x"], tab_h1, tab_x2, tab_a3][l]
                if l:
                    pool.wait_ge(stored[0], stored_all(l - 1, 0))
                    pool.wait_ge(stored[1], stored_all(l - 1, 1))
                with pool.If(general == 0):
                    for g in steps(pool, G, 0, SLOTS):
                        q = g.slot(SLOTS)
                        pool.wait_ge(idx_loaded[q], slot_value(g, l, 16))
                        pool.nop(nofuse=True)
                        gather(table, q, q, gathered[q])
                with pool.Else():
                    with pool.Fori(0, G) as i:
                        loads = 16 * slow_loads[l]
                        pool.wait_ge(slow_loaded, Step(0, i, 1).value(
                            loads, 16 * G * sum(slow_loads[:l]) + loads))
                        pool.nop(nofuse=True)
                        gather(table, 0, 0, slow_gathered)
                        if l == 3:
                            gather(tab_b3, 1, 1, slow_gathered)
                if l in (0, 2):
                    pool.wait_ge(bn_var_ready, 1 + n_tab[l])
                    pool.tensor_tensor(bnv[:, 6:7], bnv[:, 1:2], eps_row[0:D, 0:1], ALU.add).then_inc(bn_eps_added, 1)
                    pool.wait_ge(bn_eps_added, 1 + n_tab[l])
                    pool.tensor_tensor(bnv[:, 2:3], bnv[:, 6:7], neg_half[0:D, 0:1], ALU.pow
                                       ).then_inc(bn_rstd_ready, 1)
                for c in steps(pool, NCH, 0, 2):
                    b = c.slot(2)
                    pool.wait_ge(var_ready, c.value(1, l * NCH + 1))
                    pool.tensor_tensor(vare[:, b, :], mv[:, b, 1::2], eps_row[:, :], ALU.add).then_inc(eps_added, 1)
                    pool.wait_ge(eps_added, c.value(1, l * NCH + 1))
                    pool.tensor_tensor(rstd[:, b, :], vare[:, b, :], neg_half[:, :], ALU.pow
                                       ).then_inc(rstd_ready, 1)

        @block.tensor
        def _(pe):
            def window_sums(l, g, lhs):
                b = g.slot(2)
                pe.wait_ge(hot_ready, g.value(1, l * G + 1))
                pe.wait_ge(window_added, g.value(1, l * G + SLOTS - 1))
                for j in range(J):
                    mm = pe.matmul(ps[b][0:D, 0:WIN], lhs[:, j * D:(j + 1) * D],
                                   hot[:, g.slot(4), j * WIN:(j + 1) * WIN], start=(j == 0), stop=(j == J - 1))
                mm.then_inc(seg_done, 1)

            def edge_product(lhs, bank, weights):
                for j in range(J):
                    mm = pe.matmul(ps[bank][:, j * D:(j + 1) * D], lhs[:, j * P:(j + 1) * P], weights,
                                   start=True, stop=True)
                return mm

            pe.wait_ge(prep_done, 1)
            pe.wait_ge(pool_consts, 7)
            general = is_general(pe)
            for l in range(4):
                lag = [1, 0, 0, 3][l]
                with pe.If(general == 0):
                    for s in steps(pe, G, lag, SLOTS):
                        if l == 0 and s.within(G):
                            pe.wait_ge(attr_loaded[s.slot(SLOTS)], slot_value(s, 0, 16))
                            edge_product(attr[0:DE + 1, s.slot(SLOTS), :], 2 + s.slot(2), wt("We", DE + 1)
                                         ).then_inc(attr_product, 1)
                        g = s.back(1)
                        if l == 3 and g.within(G):
                            b, rs = g.slot(2), g.slot(ROWSLOTS)
                            pe.wait_ge(gathered[g.slot(SLOTS)], slot_value(g, l, 16 * J))
                            pe.wait_ge(hotT_ready, g.value(1, 1))
                            pe.matmul(ps[4 + b][0:D, :], bwin[:, rs, :], hotT[:, b, :], start=True, stop=False)
                            for j in range(J):
                                mm = pe.matmul(ps[4 + b][0:D, j * P:(j + 1) * P],
                                               gat[:, g.slot(SLOTS), j * D:(j + 1) * D], ident[:, :],
                                               start=False, stop=(j == J - 1))
                            mm.then_inc(pre_ready, 1)
                        g = s.back(2)
                        if l == 3 and g.within(G):
                            pe.wait_ge(hid_ready, g.value(1, 1))
                            edge_product(hid[:, g.slot(2), :], 2 + g.slot(2), wt("Wm2", D + 1)
                                         ).then_inc(attr_product, 1)
                        g = s.back(lag)
                        if g.within(G):
                            if l == 2:
                                pe.wait_ge(gathered[g.slot(SLOTS)], slot_value(g, l, 16 * J))
                                window_sums(l, g, gat[:, g.slot(SLOTS), :])
                            else:
                                pe.wait_ge(msg_ready, g.value(1, n_attr[l] * G + 1))
                                window_sums(l, g, msg[:, g.slot(2), :])
                with pe.Else():
                    with pe.Fori(0, G) as i:
                        g = Step(0, i, 1)
                        if l == 0:
                            loads = 16 * slow_loads[l]
                            pe.wait_ge(slow_loaded, g.value(loads, loads))
                            edge_product(attr[0:DE + 1, 0, :], 2, wt("We", DE + 1)).then_inc(slow_prod, 1)
                        if l == 3:
                            rows = 16 * slow_gathers[l]
                            pe.wait_ge(slow_gathered, g.value(rows, 16 * G * sum(slow_gathers[:l]) + rows))
                            for j in range(J):
                                for half in range(2):
                                    mm = pe.matmul(ps[4][0:D, j * P:(j + 1) * P], gat[:, half, j * D:(j + 1) * D],
                                                   ident[:, :], start=(half == 0), stop=(half == 1))
                            mm.then_inc(slow_pre, 1)
                            pe.wait_ge(slow_hid, g.value(1, 1))
                            edge_product(hid[:, 0, :], 2, wt("Wm2", D + 1)).then_inc(slow_prod, 1)
                        pe.wait_ge(slow_msg, g.value(1, l * G + 1))
                        pe.nop(nofuse=True)
                        with pe.Fori(0, NCH) as k:
                            pe.wait_ge(slow_hot, i * NCH + (k + (l * G * NCH + 1)))
                            for j in range(J):
                                mm = pe.matmul(ps[0][0:D, :], msg[:, 0, j * D:(j + 1) * D],
                                               hot_wide[:, j * CB:(j + 1) * CB], start=(j == 0), stop=(j == J - 1))
                            mm.then_inc(slow_seg, 1)
                pe.wait_ge(window_added, (l + 1) * G + SLOTS)
                if l == 0:
                    pe.wait_ge(x_loaded, 32)
                else:
                    pe.wait_ge(xc_ready, l * NCH + PRIME)
                for c in steps(pe, NCH, 1, 2):
                    if c.within(NCH):
                        chunk = bass.ds(c.value(CA), CA)
                        out = ps[c.slot(2)][0:D, 0:CA]
                        if l < 3:
                            mm = pe.matmul(out, wt(f"W1_{l}"), aggT[:, chunk], start=True, stop=True)
                        else:
                            pe.matmul(out, wt("Wu1a"), xT[:, chunk], start=True, stop=False)
                            mm = pe.matmul(out, wt("Wu1b"), aggT[:, chunk], start=False, stop=True)
                        mm.then_inc(mm1_done, 1)
                    c = c.back(1)
                    if c.within(NCH):
                        pe.wait_ge(t_ready, c.value(1, l * NCH + 1))
                        pe.wait_ge(u_ready, c.value(1, l * NCH + PRIME - 1))
                        pe.matmul(ps[2 + c.slot(2)][0:D, 0:CA], wt(f"W2_{l}" if l < 3 else "Wu2"),
                                  buf_b[:, c.slot(2), 0:CA], start=True, stop=True).then_inc(mm2_done, 1)
                for s in steps(pe, NCH, {0: 4, 1: 3, 2: 4, 3: 1}[l], 2):
                    c = s.back(1)
                    if c.within(NCH):
                        b = c.slot(2)
                        pe.wait_ge(r_ready, c.value(1, l * NCH + PRIME + 1))
                        pe.wait_ge(n_ready, c.value(1, l * NCH + PRIME - 1))
                        for j in range(J):
                            mm = pe.transpose(ps[b][:, j * D:(j + 1) * D], buf_b[:, b, j::J], ident[0:D, 0:D])
                        mm.then_inc(tr_ready, 1)
                    c = s.back(3)
                    if l < 3 and c.within(NCH):
                        b = c.slot(2)
                        pe.wait_ge(n_ready, c.value(1, l * NCH + PRIME + 1))
                        pe.wait_ge(xc_ready, c.value(1, l * NCH + PRIME - 1))
                        for j in range(J):
                            mm = pe.transpose(ps[2 + b][0:D, j * P:(j + 1) * P], nrm[:, b, j * D:(j + 1) * D],
                                              ident[:, :])
                        mm.then_inc(tx_ready, 1)
                    c = s.back(4)
                    if l in (0, 2) and c.within(NCH):
                        b = c.slot(2)
                        pe.wait_ge(xc_ready, c.value(1, l * NCH + PRIME + 1))
                        pe.wait_ge(tab_ready, c.value(1, n_tab[l] * NCH + PRIME - 1))
                        if l == 0:
                            mm = edge_product(hid[:, b, :], 4 + b, wt("Wpre", D + 1))
                        else:
                            edge_product(hid[0:D, b, :], 4 + 2 * b, wt("Wm1a"))
                            mm = edge_product(hid[0:D, b, :], 5 + 2 * b, wt("Wm1b"))
                        mm.then_inc(tabmm_done, 1)

        @block.scalar
        def _(act):
            act.wait_ge(prep_done, 1)
            general = is_general(act)
            for l in range(4):
                if l in (0, 3):
                    with act.If(general == 0):
                        for g in steps(act, G, 0, SLOTS):
                            b = g.slot(2)
                            if l == 0:
                                act.wait_ge(raw_ready, g.value(1, 1))
                                act.activation(msg[:, b, :], raw[:, b, :], ACT.Relu).then_inc(msg_ready, 1)
                            else:
                                act.wait_ge(pre_ready, g.value(1, ROWSLOTS + 1))
                                act.activation(hid[0:D, b, :], ps[4 + b][0:D, :], ACT.Relu,
                                               bias=wt("bm1")).then_inc(hid_ready, 1)
                    with act.Else():
                        if l == 3:
                            with act.Fori(0, G) as i:
                                act.wait_ge(slow_pre, i + 1)
                                act.activation(hid[0:D, 0, :], ps[4][0:D, :], ACT.Relu,
                                               bias=wt("bm1")).then_inc(slow_hid, 1)
                        else:
                            act.nop()
                f1, f2 = [(ACT.Relu, ACT.Identity), (ACT.Gelu, ACT.Gelu),
                          (ACT.Relu, ACT.Identity), (ACT.Relu, ACT.Identity)][l]
                for c in steps(act, NCH, 1, 2):
                    if c.within(NCH):
                        act.wait_ge(mm1_done, c.value(1, l * NCH + 1))
                        act.activation(buf_b[:, c.slot(2), 0:CA], ps[c.slot(2)][0:D, 0:CA], f1,
                                       bias=wt(f"b1_{l}" if l < 3 else "bu1")).then_inc(t_ready, 1)
                    c = c.back(1)
                    if c.within(NCH):
                        act.wait_ge(mm2_done, c.value(1, l * NCH + 1))
                        out = aggT[:, bass.ds(c.value(CA), CA)]
                        if l == 1:
                            act.wait_ge(u_final, c.value(1, l * NCH - 1))
                            out = buf_a[:, c.slot(2), 0:CA]
                        act.activation(out, ps[2 + c.slot(2)][0:D, 0:CA], f2,
                                       bias=wt(f"b2_{l}" if l < 3 else "bu2")).then_inc(u_ready, 1)
                if l in (0, 2):
                    act.wait_ge(bn_done, 1 + n_tab[l])
                if l == 3:
                    continue
                for s in steps(act, NCH, 3 if l == 1 else 4, 2):
                    c = s
                    if l in (0, 2) and c.within(NCH):
                        act.wait_ge(r_ready, c.value(1, l * NCH + PRIME - 1))
                        act.activation(buf_a[:, c.slot(2), :], aggT[:, bass.ds(c.value(CB), CB)],
                                       ACT.Relu, bias=bnv[:, 5:6], scale=bnv[:, 4:5]).then_inc(y_ready, 1)
                    c = s.back(3)
                    if c.within(NCH):
                        chunk = bass.ds(c.value(CB), CB)
                        act.wait_ge(tx_ready, c.value(1, l * NCH + PRIME + 1))
                        new = ps[2 + c.slot(2)][0:D, :]
                        natural = new.rearrange("d (j p) -> d p j", j=J)
                        if l in (0, 2):
                            act.activation(hid[0:D, c.slot(2), :], new, ACT.Identity)
                        if l < 2:
                            act.activation(aggT[:, chunk].rearrange("d (p j) -> d p j", j=J), natural,
                                           ACT.Identity, scale=1.0 if l == 0 else bnv[:, 7:8])
                        act.activation(xT[:, chunk].rearrange("d (p j) -> d p j", j=J), natural,
                                       ACT.Identity).then_inc(xc_ready, 1)
                    c = s.back(4)
                    if l in (0, 2) and c.within(NCH):
                        b = c.slot(2)
                        act.wait_ge(tabmm_done, c.value(1, n_tab[l] * NCH + 1))
                        act.wait_ge(stored[b], stored_before(l, c))
                        if l == 0:
                            act.activation(tabs[:, b, 0:J * D], ps[4 + b][:, 0:J * D], ACT.Gelu).then_inc(tab_ready, 1)
                        else:
                            act.activation(tabs[:, b, 0:J * D], ps[4 + 2 * b][:, 0:J * D], ACT.Identity)
                            act.activation(tabs[:, b, J * D:2 * J * D], ps[5 + 2 * b][:, 0:J * D],
                                           ACT.Identity).then_inc(tab_ready, 1)

        @block.vector
        def _(dve):
            chain = [0]

            def link(ins):
                chain[0] += 1
                ins.then_inc(prep, 1)
                dve.wait_ge(prep, chain[0])

            dve.wait_ge(dst_loaded, 32)
            link(dve.tensor_reduce(hi[0:GP, :], dst_rows_tmp, AX.X, ALU.max))
            dve.tensor_reduce(lo[0:GP, :], dst_rows_tmp, AX.X, ALU.min).then_inc(bounds_found, 1)
            dve.wait_ge(bounds_found, 1)
            dve.tensor_tensor(span[0:GP, :], hi[0:GP, :], lo[0:GP, :], ALU.subtract).then_inc(bounds_found, 1)
            dve.memset(attr[DE:DE + 1, :, :], 1.0)
            dve.memset(hid[D:D + 1, :, :], 1.0)
            link(dve.memset(aggT[:, NP:NP + WIN], 0.0))
            dve.wait_ge(bounds_loaded, 32)
            dve.wait_ge(pool_consts, 7)
            link(dve.tensor_tensor(rel[:, :].rearrange("p (g j) -> p g j", j=J),
                                   dst_cols_tmp.rearrange("p (g j) -> p g j", j=J),
                                   first_bc[:, :].unsqueeze(2).to_broadcast([P, G, J]), ALU.subtract))
            link(dve.tensor_copy(first_i[:, 0:G], first_bc[0:1, :]))
            link(dve.tensor_reduce(bnv[0:1, 0:1], spans, AX.X, ALU.max))
            link(dve.tensor_scalar(first_i[:, G:G + 1], bnv[0:1, 0:1], float(WIN), None, ALU.is_ge))
            link(dve.tensor_scalar(first_bc[:, :], first_bc[:, :], part[:, 0:1], None, ALU.add))
            dve.wait_ge(stored[0], 16)
            dve.wait_ge(stored[1], 16)
            link(dve.tensor_scalar(bnv[:, 7:8], wt("eps"), 1.0, None, ALU.add))
            dve.wait_ge(x_loaded, 32)
            for primed, by in [(window_added, SLOTS), (pre_ready, ROWSLOTS), (slow_done, 1), (u_ready, PRIME),
                               (n_ready, PRIME), (r_ready, PRIME), (tx_ready, PRIME), (xc_ready, PRIME),
                               (tab_ready, PRIME)]:
                dve.sem_inc(primed, by)
            dve.sem_inc(prep_done, 1)
            general = is_general(dve)

            def build_hot(l, g):
                dve.tensor_tensor(hot[:, g.slot(4), :].rearrange("p (j w) -> p j w", j=J),
                                  iota[:, 0:WIN].unsqueeze(1).to_broadcast([P, J, WIN]),
                                  rel[:, bass.ds(g.value(J), J)].unsqueeze(2).to_broadcast([P, J, WIN]),
                                  ALU.is_equal).then_inc(hot_ready, 1)

            def add_window(l, g):
                first = dve.value_load(first_i[0:1, bass.ds(g.value(), 1)], min_val=0, max_val=N)
                dve.wait_ge(seg_done, g.value(1, l * G + 1))
                dve.wait_ge(window_added, g.value(1, l * G + SLOTS))
                window = aggT[:, bass.ds(first, WIN)]
                dve.tensor_tensor(window, window, ps[g.slot(2)][0:D, 0:WIN], ALU.add).then_inc(window_added, 1)

            def layer_norm_stats(l, c):
                b = c.slot(2)
                dve.wait_ge(tr_ready, c.value(1, l * NCH + 1))
                dve.wait_ge(n_ready, c.value(1, l * NCH + PRIME - 1))
                for j in range(J):
                    ins = dve.bn_stats(st[:, b, 6 * j:6 * j + 6], ps[b][:, j * D:(j + 1) * D])
                ins.then_inc(stats_ready, 1)
                dve.wait_ge(stats_ready, c.value(1, l * NCH + 1))
                dve.nop(nofuse=True)
                for j in range(J):
                    ins = dve.bn_aggr(mv[:, b, 2 * j:2 * j + 2], st[:, b, 6 * j:6 * j + 6])
                ins.then_inc(var_ready, 1)

            def layer_norm(l, c):
                b = c.slot(2)
                dve.wait_ge(rstd_ready, c.value(1, l * NCH + 1))
                if l < 3:
                    dve.wait_ge(tx_ready, c.value(1, l * NCH + PRIME - 1))
                if l in (1, 3):
                    dve.wait_ge(stored[b], stored_before(l, c))
                for j in range(J):
                    ins = dve.tensor_scalar(nrm[:, b, j * D:(j + 1) * D], ps[b][:, j * D:(j + 1) * D],
                                            mv[:, b, 2 * j:2 * j + 1], rstd[:, b, j:j + 1],
                                            ALU.subtract, ALU.mult)
                ins.then_inc(n_ready, 1)

            def general_group(l, g, i):
                loads, rows = 16 * slow_loads[l], 16 * slow_gathers[l]
                dve.wait_ge(slow_loaded, g.value(loads, 16 * G * sum(slow_loads[:l]) + loads))
                dve.wait_ge(slow_gathered, g.value(rows, 16 * G * sum(slow_gathers[:l]) + rows))
                if l in (0, 3):
                    dve.wait_ge(slow_prod, g.value(1, n_prod[l] * G + 1))
                if l == 0:
                    dve.tensor_tensor(raw[:, 0, :], ps[2][:, 0:J * D], gat[:, 0, :], ALU.add).then_inc(slow_raw, 1)
                    dve.wait_ge(slow_raw, g.value(1, 1))
                    ins = dve.tensor_scalar(msg[:, 0, :], raw[:, 0, :], 0.0, None, ALU.max)
                if l == 1:
                    ins = dve.tensor_tensor(msg[:, 0, :], gat[:, 0, :], attr[:, 0, 0:J * D], ALU.mult)
                if l == 2:
                    ins = dve.tensor_copy(msg[:, 0, :], gat[:, 0, :])
                if l == 3:
                    ins = dve.tensor_tensor(msg[:, 0, :], ps[2][:, 0:J * D], attr[:, 0, 0:J * D], ALU.mult)
                ins.then_inc(slow_msg, 1)
                with dve.Fori(0, NCH) as k:
                    turn = i * NCH + (k + (l * G * NCH + 1))
                    dve.tensor_scalar(off[:, :], idx[:, 1, :], chunk0[:, bass.ds(k, 1)], None,
                                      ALU.subtract).then_inc(slow_off, 1)
                    dve.wait_ge(slow_off, turn)
                    dve.tensor_tensor(hot_wide.rearrange("p (j w) -> p j w", j=J),
                                      iota[:, :].unsqueeze(1).to_broadcast([P, J, CB]),
                                      off[:, :].unsqueeze(2).to_broadcast([P, J, CB]),
                                      ALU.is_equal).then_inc(slow_hot, 1)
                    dve.wait_ge(slow_seg, turn)
                    chunk = aggT[:, bass.ds(k * CB, CB)]
                    dve.tensor_tensor(chunk, chunk, ps[0][0:D, :], ALU.add).then_inc(slow_added, 1)
                    dve.wait_ge(slow_added, turn)
                dve.sem_inc(slow_done, 1)

            for l in range(4):
                lag = [1, 1, 1, 3][l]
                with dve.If(general == 0):
                    for s in steps(dve, G, lag, SLOTS):
                        if s.within(G):
                            q, b = s.slot(SLOTS), s.slot(2)
                            build_hot(l, s)
                            if l == 0:
                                dve.wait_ge(gathered[q], slot_value(s, l, 16 * J))
                                dve.wait_ge(attr_product, s.value(1, 1))
                                dve.tensor_tensor(raw[:, b, :], ps[2 + b][:, 0:J * D], gat[:, q, :],
                                                  ALU.add).then_inc(raw_ready, 1)
                            if l == 1:
                                dve.wait_ge(gathered[q], slot_value(s, l, 16 * J))
                                dve.wait_ge(attr_loaded[q], slot_value(s, n_attr[l], 16))
                                dve.tensor_tensor(msg[:, b, :], gat[:, q, :], attr[:, q, 0:J * D],
                                                  ALU.mult).then_inc(msg_ready, 1)
                            if l == 3:
                                rs = s.slot(ROWSLOTS)
                                dve.wait_ge(row_loaded[rs], s.uses(ROWSLOTS).value(32, 32))
                                dve.wait_ge(pre_ready, s.value(1, ROWSLOTS - 1))
                                dve.tensor_scalar(hotT[:, b, :], drow[0:WIN, rs, :],
                                                  first_bc[0:WIN, bass.ds(s.value(), 1)], None,
                                                  ALU.is_equal).then_inc(hotT_ready, 1)
                        g = s.back(2)
                        if l == 3 and g.within(G):
                            q, b = g.slot(SLOTS), g.slot(2)
                            dve.wait_ge(attr_loaded[q], slot_value(g, n_attr[l], 16))
                            dve.wait_ge(attr_product, g.value(1, G + 1))
                            dve.tensor_tensor(msg[:, b, :], ps[2 + b][:, 0:J * D], attr[:, q, 0:J * D],
                                              ALU.mult).then_inc(msg_ready, 1)
                        g = s.back(lag)
                        if g.within(G):
                            add_window(l, g)
                with dve.Else():
                    with dve.Fori(0, G) as i:
                        general_group(l, Step(0, i, 1), i)
                    dve.sem_inc(window_added, G)
                dve.wait_ge(window_added, (l + 1) * G + SLOTS)
                if l < 3:
                    for c in steps(dve, NCH, 0, 2):
                        chunk = aggT[:, bass.ds(c.value(CA), CA)]
                        dve.wait_ge(u_ready, c.value(1, l * NCH + PRIME + 1))
                        if l == 1:
                            dve.tensor_tensor(chunk, chunk, buf_a[:, c.slot(2), 0:CA], ALU.add).then_inc(u_final, 1)
                        else:
                            dve.bn_stats(bn[:, bass.ds(c.value(6), 6)], chunk).then_inc(u_final, 1)
                    dve.wait_ge(u_final, (l + 1) * NCH)
                else:
                    dve.wait_ge(u_ready, (l + 1) * NCH + PRIME)
                if l in (0, 2):
                    dve.nop(nofuse=True)
                    link(dve.bn_aggr(bnv[:, 0:2], bn[:, :]))
                    dve.sem_inc(bn_var_ready, 1)
                    dve.wait_ge(bn_rstd_ready, 1 + n_tab[l])
                    link(dve.tensor_tensor(bnv[:, 4:5], bnv[:, 2:3], wt(f"gamma_{l}"), ALU.mult))
                    link(dve.tensor_tensor(bnv[:, 3:4], bnv[:, 0:1], bnv[:, 4:5], ALU.mult))
                    dve.tensor_tensor(bnv[:, 5:6], wt(f"beta_{l}"), bnv[:, 3:4], ALU.subtract).then_inc(bn_done, 1)
                for s in steps(dve, NCH, 3, 2):
                    c = s.back(1)
                    if c.within(NCH):
                        chunk = bass.ds(c.value(CB), CB)
                        if l in (0, 2):
                            dve.wait_ge(y_ready, c.value(1, n_tab[l] * NCH + 1))
                        y = buf_a[:, c.slot(2), :] if l in (0, 2) else aggT[:, chunk]
                        dve.tensor_tensor(buf_b[:, c.slot(2), :], y, xT[:, chunk], ALU.add).then_inc(r_ready, 1)
                    c = s.back(2)
                    if c.within(NCH):
                        layer_norm_stats(l, c)
                    c = s.back(3)
                    if c.within(NCH):
                        layer_norm(l, c)
                if l == 2:
                    dve.wait_ge(xc_ready, (l + 1) * NCH + PRIME)
                    dve.wait_ge(r_ready, (l + 1) * NCH + PRIME)
                    link(dve.memset(aggT[:, :], 0.0))
                elif l < 2:
                    dve.wait_ge(xc_ready, (l + 1) * NCH + PRIME)
                    link(dve.memset(aggT[:, NP:NP + WIN], 0.0))


_NAMES = {
    "Wpre": ["L1_gnn_W_pre", "L1_gnn_b_pre"], "Wm2": ["L3_gnn_Wm2", "L3_gnn_bm2"],
    "We": ["L0_gnn_We", "L0_gnn_be"], "Wu2": ["L3_gnn_Wu2"], "bm1": ["L3_gnn_bm1"],
    "bu1": ["L3_gnn_bu1"], "bu2": ["L3_gnn_bu2"],
    **{f"{k}{n}_{l}": [f"L{l}_gnn_{k}{n}"] for l in range(3) for k in "Wb" for n in "12"},
    **{f"{k}_{l}": [f"L{l}_gnn_{k}"] for l in (0, 2) for k in ("gamma", "beta")},
}
_HALVES = {"Wm1a": ("L3_gnn_Wm1", 0), "Wm1b": ("L3_gnn_Wm1", D), "Wu1a": ("L3_gnn_Wu1", 0),
           "Wu1b": ("L3_gnn_Wu1", D)}


def layout(inputs):
    import numpy as np

    x = np.asarray(inputs["x"])
    src, dst = np.asarray(inputs["src"]), np.asarray(inputs["dst"])
    n, e = x.shape[0], src.shape[0]
    n_pad = -(-n // CB) * CB
    groups = -(-e // (GE * SLOTS)) * SLOTS
    e_pad = groups * GE

    def padded(v, rows, fill=0):
        out = np.full((rows,) + v.shape[1:], fill, v.dtype)
        out[:v.shape[0]] = v
        return out

    weights = np.zeros((P, WCOLS), x.dtype)
    for name, (at, width) in COL.items():
        if name == "eps":
            weights[:, at:at + 1] = np.asarray(inputs["L2_gnn_eps"])
        elif name in _HALVES:
            of, row = _HALVES[name]
            weights[0:D, at:at + width] = np.asarray(inputs[of])[row:row + D]
        else:
            row = 0
            for of in _NAMES[name]:
                v = np.asarray(inputs[of])
                v = v if v.ndim == 2 else v[:, None] if width == 1 else v[None, :]
                weights[row:row + v.shape[0], at:at + width] = v
                row += v.shape[0]

    xp = padded(x, n_pad)
    srcp, dstp = padded(src, e_pad), padded(dst, e_pad, n)
    ea32, ea96 = padded(np.asarray(inputs["edge_attr_32"]), e_pad), padded(np.asarray(inputs["edge_attr_96"]), e_pad)
    arrays = {
        "x": xp,
        "xT": np.ascontiguousarray(xp.T),
        "src_cols": np.ascontiguousarray(srcp.reshape(groups, P, J).transpose(1, 0, 2)).reshape(P, groups * J),
        "dst_cols": np.ascontiguousarray(dstp.reshape(groups, P, J).transpose(1, 0, 2)).reshape(P, groups * J),
        "dst_groups": dstp.reshape(groups // SLOTS, SLOTS, GE),
        "dst_rows": np.ascontiguousarray(dstp.reshape(groups, P, J).transpose(0, 2, 1)).reshape(groups, GE),
        "attr0T": np.ascontiguousarray(ea32.reshape(groups, P, J, DE).transpose(3, 0, 2, 1)).reshape(DE, e_pad),
        "attr96": ea96.reshape(groups * P, J * D),
        "weights": weights,
    }
    return arrays, n, groups, n_pad


def kernel(**inputs):
    import concourse.bacc as bacc
    from concourse.bass_utils import run_bass_kernel_spmd

    arrays, n, groups, n_pad = layout(inputs)
    nc = bacc.Bacc("TRN2", target_bir_lowering=False, num_devices=1)
    aps = {k: nc.dram_tensor(f"in_{k}", v.shape, mybir.dt.from_np(v.dtype), kind="ExternalInput").ap()
           for k, v in arrays.items()}
    aps["out"] = nc.dram_tensor("out_x", (n_pad, D), F32, kind="ExternalOutput").ap()
    build(nc, aps, n, groups)
    result = run_bass_kernel_spmd(nc, [{f"in_{k}": v for k, v in arrays.items()}], core_ids=[0])
    return result.results[0]["out_x"][:n]
```

```python
from contextlib import ExitStack

import concourse.bass as bass
from concourse import mybir

F32 = mybir.dt.float32
I32 = mybir.dt.int32
ALU = mybir.AluOpType
ACT = mybir.ActivationFunctionType
AX = mybir.AxisListType

P = 128
D = 96
DE = 32
J = 4
GE = P * J
CB = P * J
WIN = 64
STEP = dict(norm=3, back=3, new_x=3, table=4, rows=5)
SLOTS = 8
ROWSLOTS = 4
EPS = 1e-5
STAGES = 6
PRIME = 2

_BLOCKS = [("Wpre", D), ("Wm2", D), ("We", D), ("Wm1a", D), ("Wm1b", D), ("W1_0", D), ("W1_1", D),
           ("W1_2", D), ("Wu1a", D), ("Wu1b", D), ("W2_0", D), ("W2_1", D), ("W2_2", D), ("Wu2", D),
           ("b1_0", 1), ("b1_1", 1), ("b1_2", 1), ("bu1", 1), ("b2_0", 1), ("b2_1", 1), ("b2_2", 1),
           ("bu2", 1), ("gamma_0", 1), ("beta_0", 1), ("gamma_2", 1), ("beta_2", 1), ("bm1", 1),
           ("eps", 1)]
COL = {name: (sum(wd for _, wd in _BLOCKS[:k]), width) for k, (name, width) in enumerate(_BLOCKS)}
WCOLS = sum(width for _, width in _BLOCKS)


class Step:

    def __init__(self, const, i=None, stride=0):
        self.const, self.i, self.stride = const, i, stride

    def back(self, n):
        return Step(self.const - n, self.i, self.stride)

    def within(self, total):
        return self.i is not None or 0 <= self.const < total

    def value(self, scale=1, plus=0):
        if self.i is None:
            return self.const * scale + plus
        return self.i * (self.stride * scale) + (self.const * scale + plus)

    def slot(self, n):
        return self.const % n

    def uses(self, n):
        return Step(self.const // n, self.i, self.stride // n)


def steps(eng, total, lag, unroll):
    for s in range(lag):
        yield Step(s)
    loops = (total - lag) // unroll
    with eng.Fori(0, loops) as i:
        for s in range(unroll):
            yield Step(lag + s, i, unroll)
    for s in range(lag + loops * unroll, total + lag):
        yield Step(s)


def laps(eng, n_chunks, lap, lag):
    first = first_step(lap)

    def chunk(s, c):
        return (c, s - first) if 0 <= s - first < STAGES else (None, None)

    for s in range(lag):
        yield Step(s), None, None
    with eng.Fori(0, 2 * lap // SLOTS) as i:
        for s in range(SLOTS):
            yield Step(lag + s, i, SLOTS), None, None
    with eng.Fori(0, n_chunks - 2) as i:
        for s in range(lap):
            yield Step(lag + 2 * lap + s, i, lap), *chunk(s, Step(0, i, 1))
    for s in range(lap + lag):
        yield Step(n_chunks * lap + lag + s), *chunk(s, Step(n_chunks - 2))


def first_step(lap):
    return lap - STAGES


def due(l, stage, own):
    return stage is None or stage == (own if l == 3 else 0)


def build(nc, a, n_nodes, n_groups):
    N, G = n_nodes, n_groups
    NCH = -(-N // CB)
    CA = N // NCH
    NP = NCH * CB
    LAP = G // (NCH + 1)
    BEFORE = 2 * LAP + first_step(LAP) + 1
    assert CA * NCH == N and LAP * (NCH + 1) == G and LAP % (2 * SLOTS) == 0
    GP = G // 4

    with ExitStack() as ctx:
        def sb(name, shape, dt=F32):
            return ctx.enter_context(nc.sbuf_tensor(name, shape, dt))

        def sem(name):
            return ctx.enter_context(nc.semaphore(name))

        tab_h1 = nc.dram_tensor("tab_h1", (NP, D), F32, kind="Internal").ap()
        tab_x2 = nc.dram_tensor("tab_x2", (NP, D), F32, kind="Internal").ap()
        tab_a3 = nc.dram_tensor("tab_a3", (NP, D), F32, kind="Internal").ap()
        tab_b3 = nc.dram_tensor("tab_b3", (NP, D), F32, kind="Internal").ap()
        bounds_dram = nc.dram_tensor("bounds_dram", (2, G), F32, kind="Internal").ap()

        xT = sb("xT", [D, NP])
        aggT = sb("aggT", [D, NP + WIN])
        gat = sb("gat", [P, SLOTS, J * D])
        attr = sb("attr", [P, SLOTS, GE])
        idx = sb("idx", [P, SLOTS, J], I32)
        drow = sb("drow", [P, ROWSLOTS, GE], I32)
        bwin = sb("bwin", [WIN, ROWSLOTS, D])
        raw = sb("raw", [P, 2, J * D])
        msg = sb("msg", [P, 2, J * D])
        hot = sb("hot", [P, 4, J * WIN])
        hotT = sb("hotT", [WIN, 2, GE])
        hid = sb("hid", [D + 1, 2, GE])
        rel = sb("rel", [P, G * J])
        first_bc = sb("first_bc", [P, G])
        first_i = sb("first_i", [1, G + 1], I32)
        buf_a = sb("buf_a", [D, 2, CB])
        buf_b = sb("buf_b", [D, 2, CB])
        nrm = sb("nrm", [P, 2, J * D])
        iota = sb("iota", [P, CB])
        part = sb("part", [P, 1])
        chunk0 = sb("chunk0", [P, NCH])
        ident = sb("ident", [P, P])
        bn = sb("bn", [D, NCH * 6])
        bnv = sb("bnv", [D, 8])
        st = sb("st", [P, 2, J * 6])
        mv = sb("mv", [P, 2, J * 2])
        vare = sb("vare", [P, 2, J])
        rstd = sb("rstd", [P, 2, J])
        neg_half = sb("neg_half", [P, J])
        eps_row = sb("eps_row", [P, J])
        lo = sb("lo", [P, 4])
        hi = sb("hi", [P, 4])
        span = sb("span", [P, 4])
        off = sb("off", [P, J])
        table_in = sb("table_in", [D, 1])
        root = sb("root", [P, J])
        guess = sb("guess", [P, J])
        better = sb("better", [P, J])
        w = sb("w", [P, WCOLS])

        def wt(name, rows=D):
            at, width = COL[name]
            return w[0:rows, at:at + width]

        dst_rows_tmp = attr[0:GP, 0:4, :].bitcast(I32)
        tabs = drow[:, :, :].rearrange("p s e -> p (s e)").bitcast(F32)[:, 0:4 * J * D]
        tabs = tabs.rearrange("p (b e) -> p b e", b=2)
        dst_cols_tmp = drow[:, :, :].rearrange("p s e -> p (s e)")[:, 0:G * J]
        hot_wide = drow[:, :, :].rearrange("p s e -> p (s e)").bitcast(F32)
        out_y, res = buf_a[:, 0, :], buf_a[:, 1, :]
        hidden_t, hx = buf_b[:, 0, :], buf_b[:, 1, :]
        need = buf_b[0:1, :, :].rearrange("a b e -> a (b e)")
        spans = buf_a[0:1, :, :].rearrange("a b e -> a (b e)")[:, 0:G]

        MM1, MM2, TR, BACK = [4, 4, 4, 6], [5, 5, 5, 7], [0, 6, 0, 6], [2, 7, 2, None]
        ps = [ctx.enter_context(nc.psum_tensor(f"ps{i}", [P, 512], F32)) for i in range(8)]

        weights_loaded = sem("weights_loaded")
        dst_loaded = sem("dst_loaded")
        x_loaded = sem("x_loaded")
        xT_loaded = sem("xT_loaded")
        bounds_found = sem("bounds_found")
        bounds_stored = sem("bounds_stored")
        bounds_loaded = sem("bounds_loaded")
        pool_consts = sem("pool_consts")
        prep = sem("prep")
        prep_done = sem("prep_done")
        idx_loaded = [sem(f"idx_loaded{q}") for q in range(SLOTS)]
        attr_loaded = [sem(f"attr_loaded{q}") for q in range(SLOTS)]
        gathered = [sem(f"gathered{q}") for q in range(SLOTS)]
        row_loaded = [sem(f"row_loaded{q}") for q in range(ROWSLOTS)]
        attr_product = sem("attr_product")
        raw_ready = sem("raw_ready")
        msg_ready = sem("msg_ready")
        hot_ready = sem("hot_ready")
        hotT_ready = sem("hotT_ready")
        pre_ready = sem("pre_ready")
        hid_ready = sem("hid_ready")
        seg_done = sem("seg_done")
        window_added = sem("window_added")
        mm1_done = sem("mm1_done")
        t_ready = sem("t_ready")
        mm2_done = sem("mm2_done")
        u_ready = sem("u_ready")
        u_final = sem("u_final")
        bn_var_ready = sem("bn_var_ready")
        bn_eps_added = sem("bn_eps_added")
        bn_rstd_ready = sem("bn_rstd_ready")
        bn_done = sem("bn_done")
        y_ready = sem("y_ready")
        r_ready = sem("r_ready")
        tr_ready = sem("tr_ready")
        stats_ready = sem("stats_ready")
        var_ready = sem("var_ready")
        eps_added = sem("eps_added")
        rstd_ready = sem("rstd_ready")
        n_ready = sem("n_ready")
        vare_ready = sem("vare_ready")
        root_ready = sem("root_ready")
        sharpened = sem("sharpened")
        hx_ready = sem("hx_ready")
        tx_ready = sem("tx_ready")
        xc_ready = sem("xc_ready")
        hid_new = sem("hid_new")
        tabmm_done = sem("tabmm_done")
        tab_ready = sem("tab_ready")
        stored = [sem("stored0"), sem("stored1")]
        slow_loaded = [sem(f"slow_loaded{l}") for l in range(4)]
        slow_gathered = [sem(f"slow_gathered{l}") for l in range(4)]
        slow_prod = sem("slow_prod")
        slow_pre = sem("slow_pre")
        slow_hid = sem("slow_hid")
        slow_raw = sem("slow_raw")
        slow_msg = sem("slow_msg")
        slow_off = sem("slow_off")
        slow_hot = sem("slow_hot")
        slow_seg = sem("slow_seg")
        slow_added = sem("slow_added")
        slow_done = sem("slow_done")

        n_attr = {0: 0, 1: 1, 3: 2}
        n_prod = {0: 0, 3: 1}
        n_tab = {0: 0, 2: 1}
        fused = (1, 3)
        n_fused = {1: 0, 3: 1}
        per_store = [1, 1, 2, 1]
        slow_loads = [3, 3, 2, 3]
        slow_gathers = [J, J, J, 2 * J]

        def stores_of(l, b):
            if l in fused:
                return NCH * per_store[l] if b == 0 else 0
            return -(-(NCH - b) // 2) * per_store[l]

        def stored_before(l, c):
            b = 0 if l in fused else c.slot(2)
            base = 16 * (1 + sum(stores_of(k, b) for k in range(l)))
            return (c if l in fused else c.uses(2)).value(16 * per_store[l], base)

        def stored_all(l, b):
            return 16 * (1 + sum(stores_of(k, b) for k in range(l + 1)))

        def added(l, c):
            if c.i is None and c.const == NCH - 1:
                return (l + 1) * G + SLOTS
            return c.value(LAP, l * G + SLOTS + BEFORE)

        def slot_value(g, layers, per):
            return g.uses(SLOTS).value(per, per * (layers * (G // SLOTS) + 1))

        def is_general(eng):
            return eng.value_load(first_i[0:1, G:G + 1], min_val=0, max_val=1)

        block = ctx.enter_context(nc.Block())

        @block.sync
        def _(sp):
            def load_indices(l, g, early=False):
                q = g.slot(SLOTS)
                if l == 3:
                    sp.wait_ge(pre_ready, g.value(1, 1))
                elif not early:
                    sp.wait_ge(window_added, g.value(1, l * G + 1))
                sp.dma_start(idx[:, q, :], a["src_cols"][:, bass.ds(g.value(J), J)]).then_inc(idx_loaded[q], 16)

            def load_attributes(l, g, early=False):
                q = g.slot(SLOTS)
                if not early:
                    sp.wait_ge(window_added, g.value(1, l * G + 1))
                if l == 0:
                    sp.dma_start(attr[0:DE, q, :], a["attr0T"][:, bass.ds(g.value(GE), GE)]
                                 ).then_inc(attr_loaded[q], 16)
                else:
                    sp.dma_start(attr[:, q, 0:J * D], a["attr96"][bass.ds(g.value(P), P), :]
                                 ).then_inc(attr_loaded[q], 16)

            sp.dma_start(dst_rows_tmp, a["dst_groups"]).then_inc(dst_loaded, 16)
            sp.dma_start(dst_cols_tmp, a["dst_cols"]).then_inc(dst_loaded, 16)
            for g in range(SLOTS):
                load_indices(0, Step(g), True)
            half = WCOLS // 2
            sp.dma_start(w[:, 0:half], a["weights"][:, 0:half]).then_inc(stored[0], 16)
            sp.dma_start(w[:, half:WCOLS], a["weights"][:, half:WCOLS]).then_inc(stored[1], 16)
            sp.wait_ge(bounds_found, 2)
            sp.dma_start(bounds_dram[0:1, :].rearrange("a (p k) -> (a p) k", k=4), lo[0:GP, :]
                         ).then_inc(bounds_stored, 16)
            sp.dma_start(bounds_dram[1:2, :].rearrange("a (p k) -> (a p) k", k=4), span[0:GP, :]
                         ).then_inc(bounds_stored, 16)
            sp.wait_ge(bounds_stored, 32)
            sp.dma_start(first_bc[:, :], bounds_dram[0:1, :].to_broadcast([P, G])).then_inc(bounds_loaded, 16)
            sp.dma_start(spans, bounds_dram[1:2, :]).then_inc(bounds_loaded, 16)
            for g in range(SLOTS):
                load_attributes(0, Step(g), True)
            sp.dma_start(aggT[:, 0:NP], a["xT"]).then_inc(x_loaded, 16)
            sp.wait_ge(prep_done, 1)
            general = is_general(sp)

            def load_rows(g):
                rs = g.slot(ROWSLOTS)
                sp.wait_ge(pre_ready, g.value(1, SLOTS - ROWSLOTS + 1))
                sp.dma_start(drow[0:WIN, rs, :], a["dst_rows"][bass.ds(g.value(), 1), :].to_broadcast([WIN, GE])
                             ).then_inc(row_loaded[rs], 16)
                first = sp.value_load(first_i[0:1, bass.ds(g.value(), 1)], min_val=0, max_val=N)
                sp.dma_start(bwin[:, rs, :], tab_b3[bass.ds(first, WIN), :]).then_inc(row_loaded[rs], 16)

            def load_x(c):
                chunk = bass.ds(c.value(CB), CB)
                sp.dma_start(xT[:, chunk], a["xT"][:, chunk]).then_inc(xT_loaded, 16)

            def store_chunk(l, c):
                b = 0 if l in fused else c.slot(2)
                if l in fused:
                    sp.wait_ge(n_ready, c.value(1, l * NCH + PRIME + 1))
                else:
                    sp.wait_ge(tab_ready, c.value(1, n_tab[l] * NCH + PRIME + 1))
                for table, source in {
                    0: [(tab_h1, tabs[:, b, 0:J * D])],
                    1: [(tab_x2, nrm[:, b, :])],
                    2: [(tab_a3, tabs[:, b, 0:J * D]), (tab_b3, tabs[:, b, J * D:2 * J * D])],
                    3: [(a["out"], nrm[:, b, :])],
                }[l]:
                    sp.dma_start(table.rearrange("(r j) d -> r (j d)", j=J)[bass.ds(c.value(P), P), :], source
                                 ).then_inc(stored[b], 16)

            for l in range(4):
                with sp.If(general == 0):
                    sp_lag = SLOTS + 3
                    for g, c, stage in laps(sp, NCH, LAP, sp_lag):
                        early = l == 0 and g.i is None and g.const < SLOTS
                        if g.within(G) and not early:
                            load_indices(l, g)
                        g_attr, g_rows = g.back(2 if l == 3 else 0), g.back(ROWSLOTS)
                        if l != 2 and g_attr.within(G) and not early:
                            load_attributes(l, g_attr)
                        if l == 3 and g_rows.i is None and g_rows.const == 0:
                            sp.wait_ge(stored[0], stored_all(2, 0))
                            sp.wait_ge(stored[1], stored_all(2, 1))
                        if l == 3 and g_rows.within(G):
                            load_rows(g_rows)
                        if c and l == 0 and stage == 0:
                            load_x(c)
                        if c and l in fused and due(l, stage, 5):
                            store_chunk(l, c)
                with sp.Else():
                    if l == 0:
                        with sp.Fori(0, NCH - 1) as i:
                            load_x(Step(0, i, 1))
                        for q in range(2):
                            sp.wait_ge(gathered[q], 16 * J)
                            sp.wait_ge(attr_loaded[q], 16)
                    with sp.Fori(0, G) as i:
                        g = Step(0, i, 1)
                        sp.wait_ge(slow_done, g.value(1, l * G + 1))
                        sp.dma_start(idx[:, 0, :], a["src_cols"][:, bass.ds(g.value(J), J)]).then_inc(slow_loaded[l], 16)
                        sp.dma_start(idx[:, 1, :], a["dst_cols"][:, bass.ds(g.value(J), J)]).then_inc(slow_loaded[l], 16)
                        if l == 0:
                            sp.dma_start(attr[0:DE, 0, :], a["attr0T"][:, bass.ds(g.value(GE), GE)]
                                         ).then_inc(slow_loaded[l], 16)
                        if l in (1, 3):
                            sp.dma_start(attr[:, 0, 0:J * D], a["attr96"][bass.ds(g.value(P), P), :]
                                         ).then_inc(slow_loaded[l], 16)
                    if l in fused:
                        with sp.Fori(0, NCH - 1) as i:
                            store_chunk(l, Step(0, i, 1))
                if l == 0:
                    load_x(Step(NCH - 1))
                if l in fused:
                    store_chunk(l, Step(NCH - 1))
                else:
                    for c in steps(sp, NCH, 0, 2):
                        store_chunk(l, c)
            for b in range(2):
                sp.wait_ge(stored[b], stored_all(3, b))

        @block.gpsimd
        def _(pool):
            pool.iota(iota[:, :], [[1, CB]], base=0, channel_multiplier=0,
                      allow_small_or_imprecise_dtypes=True).then_inc(pool_consts, 1)
            pool.iota(chunk0[:, :], [[CB, NCH]], base=0, channel_multiplier=0,
                      allow_small_or_imprecise_dtypes=True).then_inc(pool_consts, 1)
            pool.iota(part[:, :], [[0, 1]], base=0, channel_multiplier=1,
                      allow_small_or_imprecise_dtypes=True).then_inc(pool_consts, 1)
            pool.memset(neg_half[:, :], -0.5).then_inc(pool_consts, 1)
            pool.memset(eps_row[:, :], EPS).then_inc(pool_consts, 1)
            pool.memset(need[:, 0:BEFORE], 0.0).then_inc(pool_consts, 1)
            pool.iota(need[:, BEFORE:BEFORE + (NCH - 1) * LAP], [[CB, NCH - 1], [0, LAP]], base=CB,
                      channel_multiplier=0, allow_small_or_imprecise_dtypes=True).then_inc(pool_consts, 1)
            pool.memset(ident[:, :], 0.0).then_inc(pool_consts, 1)
            pool.wait_ge(pool_consts, 8)
            pool.affine_select(out=ident[:, :], in_=ident[:, :], pattern=[[-1, P]],
                               compare_op=ALU.not_equal, fill=1.0, base=0,
                               channel_multiplier=1).then_inc(pool_consts, 1)

            def gather(table, to, indices, done):
                for j in range(J):
                    pool.indirect_dma_start(
                        out=gat[:, to, j * D:(j + 1) * D], out_offset=None, in_=table,
                        in_offset=bass.IndirectOffsetOnAxis(ap=idx[:, indices, j:j + 1], axis=0),
                    ).then_inc(done, 16)

            def gather_group(l, table, g):
                q = g.slot(SLOTS)
                pool.wait_ge(idx_loaded[q], slot_value(g, l, 16))
                pool.nop(nofuse=True)
                gather(table, q, q, gathered[q])

            for g in range(SLOTS):
                gather_group(0, a["x"], Step(g))
            pool.wait_ge(prep_done, 1)
            general = is_general(pool)
            for l in range(4):
                table = [a["x"], tab_h1, tab_x2, tab_a3][l]
                if l:
                    pool.wait_ge(stored[0], stored_all(l - 1, 0))
                    pool.wait_ge(stored[1], stored_all(l - 1, 1))
                with pool.If(general == 0):
                    with pool.Fori(0 if l else 1, G // SLOTS) as i:
                        for q in range(SLOTS):
                            gather_group(l, table, Step(q, i, SLOTS))
                with pool.Else():
                    with pool.Fori(0, G) as i:
                        loads = 16 * slow_loads[l]
                        pool.wait_ge(slow_loaded[l], Step(0, i, 1).value(loads, loads))
                        pool.nop(nofuse=True)
                        gather(table, 0, 0, slow_gathered[l])
                        if l == 3:
                            gather(tab_b3, 1, 1, slow_gathered[l])
                if l in (0, 2):
                    pool.wait_ge(bn_var_ready, 1 + n_tab[l])
                    pool.tensor_tensor(bnv[:, 6:7], bnv[:, 1:2], eps_row[0:D, 0:1], ALU.add).then_inc(bn_eps_added, 1)
                    pool.wait_ge(bn_eps_added, 1 + n_tab[l])
                    pool.tensor_tensor(bnv[:, 2:3], bnv[:, 6:7], neg_half[0:D, 0:1], ALU.pow
                                       ).then_inc(bn_rstd_ready, 1)
                    for c in steps(pool, NCH, 0, 2):
                        b = c.slot(2)
                        pool.wait_ge(var_ready, c.value(1, l * NCH + 1))
                        pool.tensor_tensor(vare[:, b, :], mv[:, b, 1::2], eps_row[:, :], ALU.add).then_inc(eps_added, 1)
                        pool.wait_ge(eps_added, c.value(1, n_tab[l] * NCH + 1))
                        pool.tensor_tensor(rstd[:, b, :], vare[:, b, :], neg_half[:, :], ALU.pow
                                           ).then_inc(rstd_ready, 1)

        @block.tensor
        def _(pe):
            def window_sums(l, g, lhs):
                b = g.slot(2)
                pe.wait_ge(hot_ready, g.value(1, l * G + 1))
                pe.wait_ge(window_added, g.value(1, l * G + SLOTS - 1))
                for j in range(J):
                    mm = pe.matmul(ps[b][0:D, 0:WIN], lhs[:, j * D:(j + 1) * D],
                                   hot[:, g.slot(4), j * WIN:(j + 1) * WIN], start=(j == 0), stop=(j == J - 1))
                mm.then_inc(seg_done, 1)

            def edge_product(lhs, bank, weights):
                for j in range(J):
                    mm = pe.matmul(ps[bank][:, j * D:(j + 1) * D], lhs[:, j * P:(j + 1) * P], weights,
                                   start=True, stop=True)
                return mm

            def mlp_chunk(l, c, stage=None):
                size = CB if l in fused else CA
                chunk = bass.ds(c.value(size), size)
                if due(l, stage, 0):
                    pe.wait_ge(window_added, added(l, c))
                    if l == 3:
                        pe.wait_ge(n_ready, c.value(1, l * NCH + PRIME))
                    out = ps[MM1[l]][0:D, 0:size]
                    if l < 3:
                        mm = pe.matmul(out, wt(f"W1_{l}"), aggT[:, chunk], start=True, stop=True)
                    else:
                        pe.matmul(out, wt("Wu1a"), xT[:, chunk], start=True, stop=False)
                        mm = pe.matmul(out, wt("Wu1b"), aggT[:, chunk], start=False, stop=True)
                    mm.then_inc(mm1_done, 1)
                if due(l, stage, 1):
                    pe.wait_ge(t_ready, c.value(1, l * NCH + 1))
                    pe.wait_ge(u_ready, c.value(1, l * NCH + PRIME))
                    pe.matmul(ps[MM2[l]][0:D, 0:size], wt(f"W2_{l}" if l < 3 else "Wu2"), hidden_t[:, 0:size],
                              start=True, stop=True).then_inc(mm2_done, 1)
                if l in fused and due(l, stage, 3):
                    pe.wait_ge(r_ready, c.value(1, l * NCH + PRIME + 1))
                    for j in range(J):
                        mm = pe.transpose(ps[TR[l]][:, j * D:(j + 1) * D], res[:, j::J], ident[0:D, 0:D])
                    mm.then_inc(tr_ready, 1)
                if l == 1 and due(l, stage, 5):
                    pe.wait_ge(n_ready, c.value(1, l * NCH + PRIME + 1))
                    pe.wait_ge(xc_ready, c.value(1, l * NCH + PRIME))
                    for j in range(J):
                        mm = pe.transpose(ps[BACK[l]][0:D, j * P:(j + 1) * P], nrm[:, 0, j * D:(j + 1) * D],
                                          ident[:, :])
                    mm.then_inc(tx_ready, 1)

            pe.wait_ge(prep_done, 1)
            pe.wait_ge(pool_consts, 9)
            general = is_general(pe)
            for l in range(4):
                lag = [1, 0, 0, 3][l]
                with pe.If(general == 0):
                    for s, c, stage in laps(pe, NCH, LAP, lag):
                        if l == 0 and s.within(G):
                            pe.wait_ge(attr_loaded[s.slot(SLOTS)], slot_value(s, 0, 16))
                            edge_product(attr[0:DE + 1, s.slot(SLOTS), :], 2 + s.slot(2), wt("We", DE + 1)
                                         ).then_inc(attr_product, 1)
                        g = s.back(1)
                        if l == 3 and g.within(G):
                            b, rs = g.slot(2), g.slot(ROWSLOTS)
                            pe.wait_ge(gathered[g.slot(SLOTS)], slot_value(g, l, 16 * J))
                            pe.wait_ge(hotT_ready, g.value(1, 1))
                            pe.matmul(ps[4 + b][0:D, :], bwin[:, rs, :], hotT[:, b, :], start=True, stop=False)
                            for j in range(J):
                                mm = pe.matmul(ps[4 + b][0:D, j * P:(j + 1) * P],
                                               gat[:, g.slot(SLOTS), j * D:(j + 1) * D], ident[:, :],
                                               start=False, stop=(j == J - 1))
                            mm.then_inc(pre_ready, 1)
                        g = s.back(2)
                        if l == 3 and g.within(G):
                            pe.wait_ge(hid_ready, g.value(1, 1))
                            edge_product(hid[:, g.slot(2), :], 2 + g.slot(2), wt("Wm2", D + 1)
                                         ).then_inc(attr_product, 1)
                        g = s.back(lag)
                        if g.within(G):
                            if l == 2:
                                pe.wait_ge(gathered[g.slot(SLOTS)], slot_value(g, l, 16 * J))
                                window_sums(l, g, gat[:, g.slot(SLOTS), :])
                            else:
                                pe.wait_ge(msg_ready, g.value(1, n_attr[l] * G + 1))
                                window_sums(l, g, msg[:, g.slot(2), :])
                        if c:
                            mlp_chunk(l, c, stage)
                with pe.Else():
                    with pe.Fori(0, G) as i:
                        g = Step(0, i, 1)
                        if l == 0:
                            loads = 16 * slow_loads[l]
                            pe.wait_ge(slow_loaded[l], g.value(loads, loads))
                            edge_product(attr[0:DE + 1, 0, :], 2, wt("We", DE + 1)).then_inc(slow_prod, 1)
                        if l == 3:
                            rows = 16 * slow_gathers[l]
                            pe.wait_ge(slow_gathered[l], g.value(rows, rows))
                            for j in range(J):
                                for half in range(2):
                                    mm = pe.matmul(ps[4][0:D, j * P:(j + 1) * P], gat[:, half, j * D:(j + 1) * D],
                                                   ident[:, :], start=(half == 0), stop=(half == 1))
                            mm.then_inc(slow_pre, 1)
                            pe.wait_ge(slow_hid, g.value(1, 1))
                            edge_product(hid[:, 0, :], 2, wt("Wm2", D + 1)).then_inc(slow_prod, 1)
                        pe.wait_ge(slow_msg, g.value(1, l * G + 1))
                        pe.nop(nofuse=True)
                        with pe.Fori(0, NCH) as k:
                            pe.wait_ge(slow_hot, i * NCH + (k + (l * G * NCH + 1)))
                            for j in range(J):
                                mm = pe.matmul(ps[0][0:D, :], msg[:, 0, j * D:(j + 1) * D],
                                               hot_wide[:, j * CB:(j + 1) * CB], start=(j == 0), stop=(j == J - 1))
                            mm.then_inc(slow_seg, 1)
                    with pe.Fori(0, NCH - 1) as i:
                        mlp_chunk(l, Step(0, i, 1))
                mlp_chunk(l, Step(NCH - 1))
                if l in fused:
                    continue

                def node_major(l, c):
                    if c.within(NCH):
                        b = c.slot(2)
                        pe.wait_ge(r_ready, c.value(1, l * NCH + PRIME + 1))
                        pe.wait_ge(n_ready, c.value(1, l * NCH + PRIME - 1))
                        for j in range(J):
                            mm = pe.transpose(ps[TR[l] + b][:, j * D:(j + 1) * D], buf_b[:, b, j::J],
                                              ident[0:D, 0:D])
                        mm.then_inc(tr_ready, 1)

                def features_major(l, c):
                    if c.within(NCH):
                        b = c.slot(2)
                        pe.wait_ge(n_ready, c.value(1, l * NCH + PRIME + 1))
                        pe.wait_ge(xc_ready, c.value(1, l * NCH + PRIME - 1))
                        for j in range(J):
                            mm = pe.transpose(ps[BACK[l] + b][0:D, j * P:(j + 1) * P],
                                              nrm[:, b, j * D:(j + 1) * D], ident[:, :])
                        mm.then_inc(tx_ready, 1)

                for s in steps(pe, NCH, STEP["table"], 2):
                    node_major(l, s.back(1))
                    features_major(l, s.back(STEP["back"]))
                    c = s.back(STEP["table"])
                    if c.within(NCH):
                        b = c.slot(2)
                        pe.wait_ge(hid_new, c.value(1, n_tab[l] * NCH + 1))
                        pe.wait_ge(tab_ready, c.value(1, n_tab[l] * NCH + PRIME - 1))
                        if l == 0:
                            mm = edge_product(hid[:, b, :], 4 + b, wt("Wpre", D + 1))
                        else:
                            for j in range(J):
                                to = (j % 2) * 2 * D
                                mm = pe.matmul(ps[4 + 2 * b + j // 2][:, to:to + 2 * D], hid[0:D, b, j * P:(j + 1) * P],
                                               w[0:D, COL["Wm1a"][0]:COL["Wm1a"][0] + 2 * D], start=True, stop=True)
                        mm.then_inc(tabmm_done, 1)

        @block.scalar
        def _(act):
            act.wait_ge(prep_done, 1)
            general = is_general(act)
            act.activation(table_in[:, :], wt("bm1"), ACT.Gelu)

            def new_x(l, c):
                if c.within(NCH):
                    chunk = bass.ds(c.value(CB), CB)
                    act.wait_ge(tx_ready, c.value(1, l * NCH + PRIME + 1))
                    new = ps[BACK[l] + (0 if l in fused else c.slot(2))][0:D, :]
                    natural = new.rearrange("d (j p) -> d p j", j=J)
                    if l in n_tab:
                        act.activation(hid[0:D, c.slot(2), :], new, ACT.Identity).then_inc(hid_new, 1)
                    if l < 2:
                        act.activation(aggT[:, chunk].rearrange("d (p j) -> d p j", j=J), natural,
                                       ACT.Identity, scale=1.0 if l == 0 else bnv[:, 7:8])
                    act.activation(xT[:, chunk].rearrange("d (p j) -> d p j", j=J), natural,
                                   ACT.Identity).then_inc(xc_ready, 1)

            def mlp_chunk(l, c, stage=None):
                size = CB if l in fused else CA
                f1, f2 = [(ACT.Relu, ACT.Identity), (ACT.Gelu, ACT.Gelu),
                          (ACT.Relu, ACT.Identity), (ACT.Relu, ACT.Identity)][l]
                if due(l, stage, 0):
                    act.wait_ge(mm1_done, c.value(1, l * NCH + 1))
                    act.activation(hidden_t[:, 0:size], ps[MM1[l]][0:D, 0:size], f1,
                                   bias=wt(f"b1_{l}" if l < 3 else "bu1")).then_inc(t_ready, 1)
                if due(l, stage, 1):
                    act.wait_ge(mm2_done, c.value(1, l * NCH + 1))
                    out = out_y if l in fused else aggT[:, bass.ds(c.value(size), size)]
                    act.activation(out, ps[MM2[l]][0:D, 0:size], f2,
                                   bias=wt(f"b2_{l}" if l < 3 else "bu2")).then_inc(u_ready, 1)
                if l in fused and due(l, stage, 4):
                    act.wait_ge(vare_ready, c.value(1, n_fused[l] * NCH + 1))
                    act.activation(root[:, :], vare[:, 0, :], ACT.Sqrt).then_inc(root_ready, 1)
                if l == 1 and due(l, stage, 5):
                    new_x(l, c)

            for l in range(4):
                with act.If(general == 0):
                    if l in (1, 2):
                        with act.Fori(0, NCH - 1) as i:
                            mlp_chunk(l, Step(0, i, 1))
                    else:
                        for g, c, stage in laps(act, NCH, LAP, 1 if l == 0 else 2):
                            b = g.slot(2)
                            if l == 0 and g.within(G):
                                act.wait_ge(raw_ready, g.value(1, 1))
                                act.activation(msg[:, b, :], raw[:, b, :], ACT.Relu).then_inc(msg_ready, 1)
                            if l == 3 and g.within(G):
                                act.wait_ge(pre_ready, g.value(1, SLOTS + 1))
                                act.activation(hid[0:D, b, :], ps[4 + b][0:D, :], ACT.Relu,
                                               bias=wt("bm1")).then_inc(hid_ready, 1)
                            if c:
                                mlp_chunk(l, c, stage)
                with act.Else():
                    if l == 3:
                        with act.Fori(0, G) as i:
                            act.wait_ge(slow_pre, i + 1)
                            act.activation(hid[0:D, 0, :], ps[4][0:D, :], ACT.Relu,
                                           bias=wt("bm1")).then_inc(slow_hid, 1)
                    with act.Fori(0, NCH - 1) as i:
                        mlp_chunk(l, Step(0, i, 1))
                mlp_chunk(l, Step(NCH - 1))
                if l in fused:
                    continue
                act.wait_ge(bn_done, 1 + n_tab[l])
                for s in steps(act, NCH, STEP["rows"], 2):
                    c = s
                    if c.within(NCH):
                        act.wait_ge(r_ready, c.value(1, l * NCH + PRIME - 1))
                        act.activation(buf_a[:, c.slot(2), :], aggT[:, bass.ds(c.value(CB), CB)],
                                       ACT.Relu, bias=bnv[:, 5:6], scale=bnv[:, 4:5]).then_inc(y_ready, 1)
                    c = s.back(STEP["rows"])
                    if c.within(NCH):
                        b = c.slot(2)
                        act.wait_ge(tabmm_done, c.value(1, n_tab[l] * NCH + 1))
                        act.wait_ge(stored[b], stored_before(l, c))
                        if l == 0:
                            act.activation(tabs[:, b, 0:J * D], ps[4 + b][:, 0:J * D], ACT.Gelu).then_inc(tab_ready, 1)
                        else:
                            rows = tabs[:, b, :].rearrange("p (t j d) -> p j t d", t=2, d=D)
                            for half in range(2):
                                ins = act.activation(
                                    rows[:, 2 * half:2 * half + 2],
                                    ps[4 + 2 * b + half][:, 0:4 * D].rearrange("p (j t d) -> p j t d", j=2, t=2),
                                    ACT.Identity)
                            ins.then_inc(tab_ready, 1)
                    new_x(l, s.back(STEP["new_x"]))

        @block.vector
        def _(dve):
            chain = [0]

            def link(ins):
                chain[0] += 1
                ins.then_inc(prep, 1)
                dve.wait_ge(prep, chain[0])

            dve.wait_ge(dst_loaded, 32)
            link(dve.tensor_reduce(hi[0:GP, :], dst_rows_tmp, AX.X, ALU.max))
            dve.tensor_reduce(lo[0:GP, :], dst_rows_tmp, AX.X, ALU.min).then_inc(bounds_found, 1)
            dve.wait_ge(bounds_found, 1)
            dve.tensor_tensor(span[0:GP, :], hi[0:GP, :], lo[0:GP, :], ALU.subtract).then_inc(bounds_found, 1)
            dve.memset(attr[DE:DE + 1, :, :], 1.0)
            dve.memset(hid[D:D + 1, :, :], 1.0)
            link(dve.memset(aggT[:, NP:NP + WIN], 0.0))
            dve.wait_ge(bounds_loaded, 32)
            dve.wait_ge(pool_consts, 9)
            link(dve.tensor_tensor(rel[:, :].rearrange("p (g j) -> p g j", j=J),
                                   dst_cols_tmp.rearrange("p (g j) -> p g j", j=J),
                                   first_bc[:, :].unsqueeze(2).to_broadcast([P, G, J]), ALU.subtract))
            link(dve.tensor_copy(first_i[:, 0:G], first_bc[0:1, :]))
            link(dve.tensor_reduce(bnv[0:1, 0:1], spans, AX.X, ALU.max))
            link(dve.tensor_scalar(bnv[0:1, 1:2], bnv[0:1, 0:1], float(WIN), None, ALU.is_ge))
            link(dve.tensor_tensor(spans, need[:, 0:G], first_bc[0:1, :], ALU.subtract))
            link(dve.tensor_reduce(bnv[0:1, 0:1], spans, AX.X, ALU.max))
            link(dve.tensor_scalar(bnv[0:1, 2:3], bnv[0:1, 0:1], 0.0, None, ALU.is_gt))
            link(dve.tensor_tensor(first_i[:, G:G + 1], bnv[0:1, 1:2], bnv[0:1, 2:3], ALU.max))
            link(dve.tensor_scalar(first_bc[:, :], first_bc[:, :], part[:, 0:1], None, ALU.add))
            dve.wait_ge(stored[0], 16)
            dve.wait_ge(stored[1], 16)
            link(dve.tensor_scalar(bnv[:, 7:8], wt("eps"), 1.0, None, ALU.add))
            for primed, by in [(window_added, SLOTS), (pre_ready, SLOTS), (slow_done, 1), (u_ready, PRIME),
                               (n_ready, PRIME), (r_ready, PRIME), (tx_ready, PRIME), (xc_ready, PRIME),
                               (tab_ready, PRIME)]:
                dve.sem_inc(primed, by)
            dve.sem_inc(prep_done, 1)
            general = is_general(dve)
            dve.wait_ge(x_loaded, 16)

            def build_hot(l, g):
                dve.tensor_tensor(hot[:, g.slot(4), :].rearrange("p (j w) -> p j w", j=J),
                                  iota[:, 0:WIN].unsqueeze(1).to_broadcast([P, J, WIN]),
                                  rel[:, bass.ds(g.value(J), J)].unsqueeze(2).to_broadcast([P, J, WIN]),
                                  ALU.is_equal).then_inc(hot_ready, 1)

            def add_window(l, g):
                first = dve.value_load(first_i[0:1, bass.ds(g.value(), 1)], min_val=0, max_val=N)
                dve.wait_ge(seg_done, g.value(1, l * G + 1))
                dve.wait_ge(window_added, g.value(1, l * G + SLOTS))
                window = aggT[:, bass.ds(first, WIN)]
                dve.tensor_tensor(window, window, ps[g.slot(2)][0:D, 0:WIN], ALU.add).then_inc(window_added, 1)

            def layer_norm_stats(l, c):
                b = 0 if l in fused else c.slot(2)
                dve.wait_ge(tr_ready, c.value(1, l * NCH + 1))
                dve.wait_ge(n_ready, c.value(1, l * NCH + PRIME - (0 if l in fused else 1)))
                for j in range(J):
                    ins = dve.bn_stats(st[:, b, 6 * j:6 * j + 6], ps[TR[l] + b][:, j * D:(j + 1) * D])
                ins.then_inc(stats_ready, 1)
                dve.wait_ge(stats_ready, c.value(1, l * NCH + 1))
                dve.nop(nofuse=True)
                for j in range(J):
                    ins = dve.bn_aggr(mv[:, b, 2 * j:2 * j + 2], st[:, b, 6 * j:6 * j + 6])
                ins.then_inc(var_ready, 1)

            def layer_norm(l, c):
                b = 0 if l in fused else c.slot(2)
                if l in fused:
                    dve.wait_ge(sharpened, c.value(SHARPEN, (n_fused[l] * NCH + 1) * SHARPEN))
                    dve.wait_ge(stored[b], stored_before(l, c))
                else:
                    dve.wait_ge(rstd_ready, c.value(1, n_tab[l] * NCH + 1))
                if l < 3:
                    dve.wait_ge(tx_ready, c.value(1, l * NCH + PRIME - (0 if l in fused else 1)))
                for j in range(J):
                    ins = dve.tensor_scalar(nrm[:, b, j * D:(j + 1) * D], ps[TR[l] + b][:, j * D:(j + 1) * D],
                                            mv[:, b, 2 * j:2 * j + 1], rstd[:, b, j:j + 1],
                                            ALU.subtract, ALU.mult)
                ins.then_inc(n_ready, 1)

            SHARPEN = 5

            def sharpened_rstd(l, c):
                first = n_fused[l] * NCH * SHARPEN
                dve.wait_ge(root_ready, c.value(1, n_fused[l] * NCH + 1))
                dve.reciprocal(guess[:, :], root[:, :]).then_inc(sharpened, 1)
                dve.wait_ge(sharpened, c.value(SHARPEN, first + 1))
                dve.tensor_tensor(better[:, :], guess[:, :], vare[:, 0, :], ALU.mult).then_inc(sharpened, 1)
                dve.wait_ge(sharpened, c.value(SHARPEN, first + 2))
                dve.tensor_tensor(better[:, :], better[:, :], guess[:, :], ALU.mult).then_inc(sharpened, 1)
                dve.wait_ge(sharpened, c.value(SHARPEN, first + 3))
                dve.tensor_scalar(better[:, :], better[:, :], -0.5, 1.5, ALU.mult, ALU.add).then_inc(sharpened, 1)
                dve.wait_ge(sharpened, c.value(SHARPEN, first + 4))
                dve.tensor_tensor(rstd[:, 0, :], guess[:, :], better[:, :], ALU.mult).then_inc(sharpened, 1)

            def node_chunk(l, c, stage=None):
                if l == 1 and due(l, stage, 0):
                    chunk = bass.ds(c.value(CB), CB)
                    dve.wait_ge(window_added, added(l, c))
                    dve.tensor_tensor(hx, xT[:, chunk], aggT[:, chunk], ALU.add).then_inc(hx_ready, 1)
                if l in n_tab and due(l, stage, 0):
                    dve.wait_ge(u_ready, c.value(1, l * NCH + PRIME + 1))
                    dve.bn_stats(bn[:, bass.ds(c.value(6), 6)], aggT[:, bass.ds(c.value(CA), CA)]
                                 ).then_inc(u_final, 1)
                if l in fused and due(l, stage, 2):
                    dve.wait_ge(u_ready, c.value(1, l * NCH + PRIME + 1))
                    other = xT[:, bass.ds(c.value(CB), CB)]
                    if l == 1:
                        dve.wait_ge(hx_ready, c.value(1, 1))
                        other = hx
                    dve.tensor_tensor(res, out_y, other, ALU.add).then_inc(r_ready, 1)
                if l in fused and due(l, stage, 4):
                    layer_norm_stats(l, c)
                    dve.wait_ge(var_ready, c.value(1, l * NCH + 1))
                    dve.tensor_scalar(vare[:, 0, :], mv[:, 0, 1::2], EPS, None, ALU.add).then_inc(vare_ready, 1)
                if l in fused and due(l, stage, 5):
                    sharpened_rstd(l, c)
                    layer_norm(l, c)

            def general_group(l, g, i):
                loads, rows = 16 * slow_loads[l], 16 * slow_gathers[l]
                dve.wait_ge(slow_loaded[l], g.value(loads, loads))
                dve.wait_ge(slow_gathered[l], g.value(rows, rows))
                if l in (0, 3):
                    dve.wait_ge(slow_prod, g.value(1, n_prod[l] * G + 1))
                if l == 0:
                    dve.tensor_tensor(raw[:, 0, :], ps[2][:, 0:J * D], gat[:, 0, :], ALU.add).then_inc(slow_raw, 1)
                    dve.wait_ge(slow_raw, g.value(1, 1))
                    ins = dve.tensor_scalar(msg[:, 0, :], raw[:, 0, :], 0.0, None, ALU.max)
                if l == 1:
                    ins = dve.tensor_tensor(msg[:, 0, :], gat[:, 0, :], attr[:, 0, 0:J * D], ALU.mult)
                if l == 2:
                    ins = dve.tensor_copy(msg[:, 0, :], gat[:, 0, :])
                if l == 3:
                    ins = dve.tensor_tensor(msg[:, 0, :], ps[2][:, 0:J * D], attr[:, 0, 0:J * D], ALU.mult)
                ins.then_inc(slow_msg, 1)
                with dve.Fori(0, NCH) as k:
                    turn = i * NCH + (k + (l * G * NCH + 1))
                    dve.tensor_scalar(off[:, :], idx[:, 1, :], chunk0[:, bass.ds(k, 1)], None,
                                      ALU.subtract).then_inc(slow_off, 1)
                    dve.wait_ge(slow_off, turn)
                    dve.tensor_tensor(hot_wide.rearrange("p (j w) -> p j w", j=J),
                                      iota[:, :].unsqueeze(1).to_broadcast([P, J, CB]),
                                      off[:, :].unsqueeze(2).to_broadcast([P, J, CB]),
                                      ALU.is_equal).then_inc(slow_hot, 1)
                    dve.wait_ge(slow_seg, turn)
                    chunk = aggT[:, bass.ds(k * CB, CB)]
                    dve.tensor_tensor(chunk, chunk, ps[0][0:D, :], ALU.add).then_inc(slow_added, 1)
                    dve.wait_ge(slow_added, turn)
                dve.sem_inc(slow_done, 1)

            for l in range(4):
                lag = [1, 1, 1, 3][l]
                with dve.If(general == 0):
                    for s, c, stage in laps(dve, NCH, LAP, lag):
                        if s.within(G):
                            q, b = s.slot(SLOTS), s.slot(2)
                            build_hot(l, s)
                            if l == 0:
                                dve.wait_ge(gathered[q], slot_value(s, l, 16 * J))
                                dve.wait_ge(attr_product, s.value(1, 1))
                                dve.tensor_tensor(raw[:, b, :], ps[2 + b][:, 0:J * D], gat[:, q, :],
                                                  ALU.add).then_inc(raw_ready, 1)
                            if l == 1:
                                dve.wait_ge(gathered[q], slot_value(s, l, 16 * J))
                                dve.wait_ge(attr_loaded[q], slot_value(s, n_attr[l], 16))
                                dve.tensor_tensor(msg[:, b, :], gat[:, q, :], attr[:, q, 0:J * D],
                                                  ALU.mult).then_inc(msg_ready, 1)
                            if l == 3:
                                rs = s.slot(ROWSLOTS)
                                dve.wait_ge(row_loaded[rs], s.uses(ROWSLOTS).value(32, 32))
                                dve.wait_ge(pre_ready, s.value(1, SLOTS - 1))
                                dve.tensor_scalar(hotT[:, b, :], drow[0:WIN, rs, :],
                                                  first_bc[0:WIN, bass.ds(s.value(), 1)], None,
                                                  ALU.is_equal).then_inc(hotT_ready, 1)
                        g = s.back(2)
                        if l == 3 and g.within(G):
                            q, b = g.slot(SLOTS), g.slot(2)
                            dve.wait_ge(attr_loaded[q], slot_value(g, n_attr[l], 16))
                            dve.wait_ge(attr_product, g.value(1, G + 1))
                            dve.tensor_tensor(msg[:, b, :], ps[2 + b][:, 0:J * D], attr[:, q, 0:J * D],
                                              ALU.mult).then_inc(msg_ready, 1)
                        g = s.back(lag)
                        if g.within(G):
                            add_window(l, g)
                        if c:
                            node_chunk(l, c, stage)
                with dve.Else():
                    with dve.Fori(0, G) as i:
                        general_group(l, Step(0, i, 1), i)
                    dve.sem_inc(window_added, G)
                    with dve.Fori(0, NCH - 1) as i:
                        node_chunk(l, Step(0, i, 1))
                node_chunk(l, Step(NCH - 1))
                if l in n_tab:
                    dve.wait_ge(u_final, (n_tab[l] + 1) * NCH)
                    dve.nop(nofuse=True)
                    link(dve.bn_aggr(bnv[:, 0:2], bn[:, :]))
                    dve.sem_inc(bn_var_ready, 1)
                    dve.wait_ge(bn_rstd_ready, 1 + n_tab[l])
                    link(dve.tensor_tensor(bnv[:, 4:5], bnv[:, 2:3], wt(f"gamma_{l}"), ALU.mult))
                    link(dve.tensor_tensor(bnv[:, 3:4], bnv[:, 0:1], bnv[:, 4:5], ALU.mult))
                    dve.tensor_tensor(bnv[:, 5:6], wt(f"beta_{l}"), bnv[:, 3:4], ALU.subtract).then_inc(bn_done, 1)
                if l == 0:
                    dve.wait_ge(xT_loaded, 16 * NCH)
                for s in [] if l in fused else steps(dve, NCH, STEP["norm"], 2):
                    c = s.back(1)
                    if c.within(NCH):
                        dve.wait_ge(y_ready, c.value(1, n_tab[l] * NCH + 1))
                        dve.tensor_tensor(buf_b[:, c.slot(2), :], buf_a[:, c.slot(2), :],
                                          xT[:, bass.ds(c.value(CB), CB)], ALU.add).then_inc(r_ready, 1)
                    c = s.back(2)
                    if c.within(NCH):
                        layer_norm_stats(l, c)
                    c = s.back(STEP["norm"])
                    if c.within(NCH):
                        layer_norm(l, c)
                if l == 2:
                    dve.wait_ge(xc_ready, (l + 1) * NCH + PRIME)
                    dve.wait_ge(r_ready, (l + 1) * NCH + PRIME)
                    link(dve.memset(aggT[:, :], 0.0))
                elif l < 2:
                    dve.wait_ge(xc_ready, (l + 1) * NCH + PRIME)
                    link(dve.memset(aggT[:, NP:NP + WIN], 0.0))


_NAMES = {
    "Wpre": ["L1_gnn_W_pre", "L1_gnn_b_pre"], "Wm2": ["L3_gnn_Wm2", "L3_gnn_bm2"],
    "We": ["L0_gnn_We", "L0_gnn_be"], "Wu2": ["L3_gnn_Wu2"], "bm1": ["L3_gnn_bm1"],
    "bu1": ["L3_gnn_bu1"], "bu2": ["L3_gnn_bu2"],
    **{f"{k}{n}_{l}": [f"L{l}_gnn_{k}{n}"] for l in range(3) for k in "Wb" for n in "12"},
    **{f"{k}_{l}": [f"L{l}_gnn_{k}"] for l in (0, 2) for k in ("gamma", "beta")},
}
_HALVES = {"Wm1a": ("L3_gnn_Wm1", 0), "Wm1b": ("L3_gnn_Wm1", D), "Wu1a": ("L3_gnn_Wu1", 0),
           "Wu1b": ("L3_gnn_Wu1", D)}


def layout(inputs):
    import numpy as np

    x = np.asarray(inputs["x"])
    src, dst = np.asarray(inputs["src"]), np.asarray(inputs["dst"])
    n, e = x.shape[0], src.shape[0]
    n_pad = -(-n // CB) * CB
    groups = -(-e // (GE * SLOTS)) * SLOTS
    e_pad = groups * GE

    def padded(v, rows, fill=0):
        out = np.full((rows,) + v.shape[1:], fill, v.dtype)
        out[:v.shape[0]] = v
        return out

    weights = np.zeros((P, WCOLS), x.dtype)
    for name, (at, width) in COL.items():
        if name == "eps":
            weights[:, at:at + 1] = np.asarray(inputs["L2_gnn_eps"])
        elif name in _HALVES:
            of, row = _HALVES[name]
            weights[0:D, at:at + width] = np.asarray(inputs[of])[row:row + D]
        else:
            row = 0
            for of in _NAMES[name]:
                v = np.asarray(inputs[of])
                v = v if v.ndim == 2 else v[:, None] if width == 1 else v[None, :]
                weights[row:row + v.shape[0], at:at + width] = v
                row += v.shape[0]

    xp = padded(x, n_pad)
    srcp, dstp = padded(src, e_pad), padded(dst, e_pad, n)
    ea32, ea96 = padded(np.asarray(inputs["edge_attr_32"]), e_pad), padded(np.asarray(inputs["edge_attr_96"]), e_pad)
    arrays = {
        "x": xp,
        "xT": np.ascontiguousarray(xp.T),
        "src_cols": np.ascontiguousarray(srcp.reshape(groups, P, J).transpose(1, 0, 2)).reshape(P, groups * J),
        "dst_cols": np.ascontiguousarray(dstp.reshape(groups, P, J).transpose(1, 0, 2)).reshape(P, groups * J),
        "dst_groups": dstp.reshape(groups // 4, 4, GE),
        "dst_rows": np.ascontiguousarray(dstp.reshape(groups, P, J).transpose(0, 2, 1)).reshape(groups, GE),
        "attr0T": np.ascontiguousarray(ea32.reshape(groups, P, J, DE).transpose(3, 0, 2, 1)).reshape(DE, e_pad),
        "attr96": ea96.reshape(groups * P, J * D),
        "weights": weights,
    }
    return arrays, n, groups, n_pad


def kernel(**inputs):
    import concourse.bacc as bacc
    from concourse.bass_utils import run_bass_kernel_spmd

    arrays, n, groups, n_pad = layout(inputs)
    nc = bacc.Bacc("TRN2", target_bir_lowering=False, num_devices=1)
    aps = {k: nc.dram_tensor(f"in_{k}", v.shape, mybir.dt.from_np(v.dtype), kind="ExternalInput").ap()
           for k, v in arrays.items()}
    aps["out"] = nc.dram_tensor("out_x", (n_pad, D), F32, kind="ExternalOutput").ap()
    build(nc, aps, n, groups)
    result = run_bass_kernel_spmd(nc, [{f"in_{k}": v for k, v in arrays.items()}], core_ids=[0])
    return result.results[0]["out_x"][:n]
```
